# Optimizing a Trainium2 kernel written in Bass

```python
import numpy as np
import jax
import jax.numpy as jnp

def _softmax(x, axis=-1):
    return jax.nn.softmax(x, axis=axis)

def _gelu(x):
    return jax.nn.gelu(x, approximate=True)

def _silu(x):
    return jax.nn.silu(x)

def _sigmoid(x):
    return jax.nn.sigmoid(x)

def _layernorm(x, axis=-1, eps=1e-05):
    m = jnp.mean(x, axis=axis, keepdims=True)
    v = jnp.var(x, axis=axis, keepdims=True)
    return (x - m) / jnp.sqrt(v + eps)

def _scatter_add(tgt, idx, src, axis=0):
    return tgt.at[idx].add(src)

def _segment_sum(src, seg, n):
    return jax.ops.segment_sum(src, seg, n)
kernel_name = 'mk_perceiver_d1_seqx_r4_5e67eb'

def setup_inputs(seed: int=0):
    np.random.seed(seed)
    _w = jnp.asarray

    def _rec_inputs():
        import jax
        import jax.numpy as jnp
        _rk = jax.random.key(seed)
        x = -0.0003929 + 0.9999 * jax.random.normal(jax.random.fold_in(_rk, 1), (1, 128, 256), jnp.float32)
        _lenS = 128 - jax.random.randint(jax.random.fold_in(_rk, 7), (1,), 0, max(1, 128 // 4) + 1, jnp.int32)
        _lenS2 = 12544 - jax.random.randint(jax.random.fold_in(_rk, 8), (1,), 0, max(1, 12544 // 4) + 1, jnp.int32)
        _ctx_1024P = jax.random.normal(jax.random.fold_in(_rk, 11), (1, 16, 256), jnp.float32)
        _ctx_1024c = jax.random.dirichlet(jax.random.fold_in(_rk, 511), 0.3 * jnp.ones((16,), jnp.float32), (1, 12544))
        _ctx_1024t = jnp.einsum('bsk,bkd->bsd', _ctx_1024c, _ctx_1024P)
        _ctx_1024t = _ctx_1024t * jax.lax.rsqrt(jnp.mean(jnp.square(_ctx_1024t)) + 1e-12) * 0.953939
        ctx_1024 = -0.000514642 + 1.00011 * (_ctx_1024t + 0.3 * jax.random.normal(jax.random.fold_in(_rk, 611), (1, 12544, 256), jnp.float32))
        return (x, ctx_1024)
    x, ctx_1024 = _rec_inputs()

    def _L0_xattn_setup():
        import jax, jax.numpy as jnp
        import numpy as np
        DIM = 256
        H = 16
        DH = 64
        INNER = H * DH
        SCALE = DH ** (-0.5)
        key = jax.random.key(seed)
        ks = jax.random.split(key, 6)
        B, L, R = (4, 1024, 128)
        x = jax.random.normal(ks[0], (B, L, DIM), dtype=jnp.float32)
        context = jax.random.normal(ks[1], (B, R, DIM), dtype=jnp.float32)
        s = DIM ** (-0.5)
        Wq = jax.random.normal(ks[2], (DIM, INNER), dtype=jnp.float32) * s
        Wk = jax.random.normal(ks[3], (DIM, INNER), dtype=jnp.float32) * s
        Wv = jax.random.normal(ks[4], (DIM, INNER), dtype=jnp.float32) * s
        Wo = jax.random.normal(ks[5], (INNER, DIM), dtype=jnp.float32) * INNER ** (-0.5)
        return {'x': x, 'context': context, 'Wq': Wq, 'Wk': Wk, 'Wv': Wv, 'Wo': Wo}
    _L0_xattn_all = _L0_xattn_setup()
    _L0_xattn_in = {k: v for k, v in _L0_xattn_all.items() if k in ('Wq', 'Wk', 'Wv', 'Wo')}
    del _L0_xattn_all

    def _L0_attn_setup():
        import jax, jax.numpy as jnp
        import numpy as np
        B, N, D = (4, 1024, 256)
        H, F = (16, 128)
        HD = D // H
        key = jax.random.key(seed)
        k1, k2, k3, k4, k5 = jax.random.split(key, 5)
        x = jax.random.normal(k1, (B, N, D), dtype=jnp.float32)
        W_qkv = jax.random.normal(k2, (3 * D, D), dtype=jnp.float32) * np.sqrt(2.0 / D)
        proj = jax.random.normal(k3, (H, HD, F), dtype=jnp.float32) / np.sqrt(HD)
        W_out = jax.random.normal(k4, (D, D), dtype=jnp.float32) * np.sqrt(2.0 / D)
        b_out = jnp.zeros((D,), dtype=jnp.float32)
        return {'x': x, 'W_qkv': W_qkv, 'proj': proj, 'W_out': W_out, 'b_out': b_out}
    _L0_attn_all = _L0_attn_setup()
    _L0_attn_in = {k: v for k, v in _L0_attn_all.items() if k in ('W_qkv', 'proj', 'W_out', 'b_out')}
    del _L0_attn_all

    def _L0_ffn_setup():
        import jax, jax.numpy as jnp
        import numpy as np
        import math
        D_MODEL = 256
        N_EXPERTS = 16
        D_FF = 1024
        CAP_FACTOR = 1.25
        MIN_CAPACITY = 4

        def _capacity(num_tokens, num_experts):
            cap = math.floor(CAP_FACTOR * num_tokens / num_experts)
            cap += cap % 2
            return max(cap, MIN_CAPACITY)

        def _top1_router(gate_logits, capacity):
            s, e = gate_logits.shape
            probs = jax.nn.softmax(gate_logits, axis=-1)
            top1 = jnp.argmax(gate_logits, axis=-1)
            mask = jax.nn.one_hot(top1, e, dtype=jnp.int32)
            ranks = jnp.cumsum(mask, axis=0) - 1
            mask = mask * (ranks < capacity).astype(jnp.int32)
            rank1 = jnp.sum(mask * ranks, axis=-1)
            ranks_oh = jax.nn.one_hot(rank1, capacity, dtype=probs.dtype)
            weight = mask.astype(probs.dtype) * probs
            combine_weights = weight[:, :, None] * ranks_oh[:, None, :]
            sec_mask = combine_weights > 0
            return (combine_weights, sec_mask)
        key = jax.random.key(seed)
        k1, k2, k3, k4 = jax.random.split(key, 4)
        x = jax.random.normal(k1, (4, 512, D_MODEL), dtype=jnp.float32)
        gate_w = jax.random.normal(k2, (N_EXPERTS, D_MODEL), dtype=jnp.float32) * math.sqrt(0.1 / D_MODEL)
        w1 = jax.random.normal(k3, (N_EXPERTS, D_MODEL, D_FF), dtype=jnp.float32) * (1.0 / math.sqrt(D_MODEL))
        w2 = jax.random.normal(k4, (N_EXPERTS, D_FF, D_MODEL), dtype=jnp.float32) * (1.0 / math.sqrt(D_FF))
        return {'x': x, 'gate_w': gate_w, 'w1': w1, 'w2': w2}
    _L0_ffn_all = _L0_ffn_setup()
    _L0_ffn_in = {k: v for k, v in _L0_ffn_all.items() if k in ('gate_w', 'w1', 'w2')}
    del _L0_ffn_all
    return {'x': x, 'ctx_1024': ctx_1024, 'L0_xattn_Wq': _L0_xattn_in['Wq'], 'L0_xattn_Wk': _L0_xattn_in['Wk'], 'L0_xattn_Wv': _L0_xattn_in['Wv'], 'L0_xattn_Wo': _L0_xattn_in['Wo'], 'L0_attn_W_qkv': _L0_attn_in['W_qkv'], 'L0_attn_proj': _L0_attn_in['proj'], 'L0_attn_W_out': _L0_attn_in['W_out'], 'L0_attn_b_out': _L0_attn_in['b_out'], 'L0_ffn_gate_w': _L0_ffn_in['gate_w'], 'L0_ffn_w1': _L0_ffn_in['w1'], 'L0_ffn_w2': _L0_ffn_in['w2']}

def reference(x, ctx_1024, L0_xattn_Wq, L0_xattn_Wk, L0_xattn_Wv, L0_xattn_Wo, L0_attn_W_qkv, L0_attn_proj, L0_attn_W_out, L0_attn_b_out, L0_ffn_gate_w, L0_ffn_w1, L0_ffn_w2):
    import jax
    import jax.numpy as jnp

    def _L0_xattn_ref(x, context, Wq, Wk, Wv, Wo):
        import jax, jax.numpy as jnp
        import numpy as np
        DIM = 256
        H = 16
        DH = 64
        INNER = H * DH
        SCALE = DH ** (-0.5)
        B, L, _ = x.shape
        R = context.shape[1]
        q = (x @ Wq).reshape(B, L, H, DH).transpose(0, 2, 1, 3)
        k = (context @ Wk).reshape(B, R, H, DH).transpose(0, 2, 1, 3)
        v = (context @ Wv).reshape(B, R, H, DH).transpose(0, 2, 1, 3)
        scores = jnp.einsum('bhld,bhrd->bhlr', q, k) * SCALE
        attn = jax.nn.softmax(scores, axis=-1)
        out = jnp.einsum('bhlr,bhrd->bhld', attn, v)
        out = out.transpose(0, 2, 1, 3).reshape(B, L, INNER)
        return out @ Wo

    def _L0_attn_ref(x, W_qkv, proj, W_out, b_out):
        import jax, jax.numpy as jnp
        import numpy as np
        B, N, D = (4, 1024, 256)
        H, F = (16, 128)
        HD = D // H
        b, n, d = x.shape
        qkv = x @ W_qkv.T
        q, k, v = jnp.split(qkv, 3, axis=-1)
        reshp = lambda t: t.reshape(b, n, H, HD).transpose(0, 2, 1, 3)
        q, k, v = (reshp(q), reshp(k), reshp(v))
        q_p = jax.nn.elu(jnp.einsum('bhnd,hdf->bhnf', q, proj)) + 1.0
        k_p = jax.nn.elu(jnp.einsum('bhnd,hdf->bhnf', k, proj)) + 1.0
        kv = jnp.einsum('bhnf,bhnd->bhfd', k_p, v)
        attn = jnp.einsum('bhnf,bhfd->bhnd', q_p, kv)
        k_sum = k_p.sum(axis=2)
        z = 1.0 / (jnp.einsum('bhnf,bhf->bhn', q_p, k_sum) + 1e-08)
        attn = attn * z[..., None]
        attn = attn.transpose(0, 2, 1, 3).reshape(b, n, d)
        return attn @ W_out.T + b_out

    def _L0_ffn_ref(x, gate_w, w1, w2):
        import jax, jax.numpy as jnp
        import numpy as np
        import math
        D_MODEL = 256
        N_EXPERTS = 16
        D_FF = 1024
        CAP_FACTOR = 1.25
        MIN_CAPACITY = 4

        def _capacity(num_tokens, num_experts):
            cap = math.floor(CAP_FACTOR * num_tokens / num_experts)
            cap += cap % 2
            return max(cap, MIN_CAPACITY)

        def _top1_router(gate_logits, capacity):
            s, e = gate_logits.shape
            probs = jax.nn.softmax(gate_logits, axis=-1)
            top1 = jnp.argmax(gate_logits, axis=-1)
            mask = jax.nn.one_hot(top1, e, dtype=jnp.int32)
            ranks = jnp.cumsum(mask, axis=0) - 1
            mask = mask * (ranks < capacity).astype(jnp.int32)
            rank1 = jnp.sum(mask * ranks, axis=-1)
            ranks_oh = jax.nn.one_hot(rank1, capacity, dtype=probs.dtype)
            weight = mask.astype(probs.dtype) * probs
            combine_weights = weight[:, :, None] * ranks_oh[:, None, :]
            sec_mask = combine_weights > 0
            return (combine_weights, sec_mask)
        tokens = x.reshape(-1, D_MODEL)
        s = tokens.shape[0]
        capacity = _capacity(s, N_EXPERTS)
        gate_logits = tokens.astype(jnp.float32) @ gate_w.T
        combine_weights, sec_mask = _top1_router(gate_logits, capacity)
        dispatch = jnp.einsum('sec,sd->ecd', sec_mask.astype(tokens.dtype), tokens)
        h = jax.nn.gelu(jnp.einsum('ecd,edf->ecf', dispatch, w1))
        expert_out = jnp.einsum('ecf,efd->ecd', h, w2)
        out = jnp.einsum('sec,ecd->sd', combine_weights.astype(tokens.dtype), expert_out)
        return out.reshape(x.shape)
    x = x + _L0_xattn_ref(_layernorm(x, axis=-1), ctx_1024, L0_xattn_Wq, L0_xattn_Wk, L0_xattn_Wv, L0_xattn_Wo)
    x = x + _L0_attn_ref(_layernorm(x, axis=-1), L0_attn_W_qkv, L0_attn_proj, L0_attn_W_out, L0_attn_b_out)
    x = x + _L0_ffn_ref(_layernorm(x, axis=-1), L0_ffn_gate_w, L0_ffn_w1, L0_ffn_w2)
    return x

_drawn_inputs = setup_inputs


def setup_inputs(seed=0):
    import zlib

    import numpy as np

    out = dict(_drawn_inputs(seed))
    spreads = {'L0_attn_b_out': (0.0, 0.1)}
    factors = {'L0_attn_proj': 5.269}
    for name, (base, spread) in spreads.items():
        noise = np.random.default_rng([zlib.crc32(name.encode()), seed]).standard_normal(out[name].shape)
        drawn = base * np.exp(spread * noise) if base else spread * noise
        out[name] = jnp.asarray(drawn.astype(out[name].dtype))
    for name, factor in factors.items():
        out[name] = (out[name] * factor).astype(out[name].dtype)
    return out
```

```python
from contextlib import ExitStack

import concourse.bass as bass
from concourse import mybir

ALU = mybir.AluOpType
ACT = mybir.ActivationFunctionType
AX_X = mybir.AxisListType.X
F32 = mybir.dt.float32
F32R = mybir.dt.float32r
F16 = mybir.dt.float16
I32 = mybir.dt.int32
RMAX = bass.bass_isa.ReduceOp.max

P = 128
D = 256
KH = D // P
H = 16
DH = 64
INNER = H * DH
HP = H // 2
HD = D // H
F = 128
BANK = 512
GH = BANK // P
NG = H // GH
CT = 7
VW = DH + 2
AH = 7
VS = HD + 2
NE = 16
FF = 1024
FT = FF // P
CAP = 10
CS = 32
QE = P // CS
NQ = NE // QE
LOG_PSCALE = 11 * 0.6931471805599453
SCALE = DH ** -0.5
EPS = 1e-5
GELU_A = 0.7978845608028654
GELU_B = 0.044715
UNITS = 6


def perceiver_layer(nc, x, ctx_in, Wq, Wk, Wv, Wo, W_qkv, proj, W_out, b_out, gate_w, w1, w2, out):
    R = ctx_in.shape[1]
    NT = R // P
    NC = NT // CT
    assert R % (P * CT) == 0 and NC % 2 == 0 and NT % 2 == 0 and x.shape[1] == P
    assert CAP == max(int(1.25 * P / NE) + int(1.25 * P / NE) % 2, 4)

    with ExitStack() as ctx:
        def sb(name, shape, dt=F32):
            return ctx.enter_context(nc.sbuf_tensor(name, shape, dt))

        def sem(name):
            return ctx.enter_context(nc.semaphore(name))

        spill = nc.dram_tensor("ctxT_split", [NT, P, 2 * KH * P], F32, kind="Internal").ap()

        bank = [ctx.enter_context(nc.psum_tensor(f"pair{i}", [P, 2, BANK], F32)) for i in range(4)]

        def bk(i, n=BANK):
            return bank[i // 2][:, i % 2, 0:n]

        ident = sb("ident", [P, P])
        upper = sb("upper", [P, P])
        ones = sb("ones", [P, P])
        iota_i = sb("iota_i", [P, CS], I32)
        iota_f = sb("iota_f", [P, CS])
        zeros16 = sb("zeros16", [P, BANK], F16)
        A_hi = sb("A_hi", [P, KH, H * P], F32R)
        A_lo = sb("A_lo", [P, KH, H * P], F32R)
        Wv_hi = sb("Wv_hi", [P, KH, INNER], F32R)
        Wv_lo = sb("Wv_lo", [P, KH, INNER], F32R)
        cT = [sb(f"cT{b}", [P, 2, KH, P], F32R) for b in range(2)]
        ctxT = [sb(f"ctxT{b}", [P, CT, 2, KH, P], F32R) for b in range(2)]
        mrow = sb("mrow", [P, H * P])
        dbufs = sb("dbufs", [P, 2, BANK])
        pfulls = sb("pfulls", [P, 2, BANK])
        dbuf = [dbufs[:, i, :] for i in range(2)]
        pfull = [pfulls[:, i, :] for i in range(2)]
        P_hi = [sb(f"P_hi{b}", [P, H * P], F16) for b in range(2)]
        P_lo = [sb(f"P_lo{b}", [P, H * P], F16) for b in range(2)]
        V_hi = [sb(f"V_hi{b}", [P, H, VW], F16) for b in range(2)]
        V_lo = [sb(f"V_lo{b}", [P, H, VW], F16) for b in range(2)]
        unit = [sb(f"unit{i}", [P, KH * FF]) for i in range(UNITS)]
        Wq_sb = unit[0][:, :].rearrange("p (k n) -> p k n", k=KH)
        Wk_sb = unit[1][:, :].rearrange("p (k n) -> p k n", k=KH)
        Wv_sb = unit[2][:, :].rearrange("p (k n) -> p k n", k=KH)
        WkT = unit[3][:, :].rearrange("p (j k) -> p j k", j=HP)
        raw = [unit[4 + b][:, 0:CT * D].rearrange("p (j k) -> p j k", j=CT) for b in range(2)]
        Wo_sb = sb("Wo_sb", [P, HP, D])
        Wqkv_sb = [P_lo[r // 4][:, :].bitcast(F32)[:, (r % 4) * D:(r % 4 + 1) * D] for r in range(6)]
        WqkvT = sb("WqkvT", [P, KH, 3 * D])
        Wout_sb = [P_lo[1][:, :].bitcast(F32)[:, r * D:(r + 1) * D] for r in (2, 3)]
        WoutT = sb("WoutT", [P, KH, D])
        gate_sb = V_lo[0][:, :, :].rearrange("p h d -> p (h d)").bitcast(F32)[0:NE, 0:D]
        gateT = sb("gateT", [P, KH, NE])
        bd = sb("bd", [P, KH, 8 * F])
        b_sb = sb("b_sb", [1, D])
        x_sb = sb("x_sb", [P, D])
        xn = sb("xn", [P, D])
        xnT = sb("xnT", [P, KH, P])
        qT = dbufs[:, :, :].rearrange("p a (j l) -> p (a j) l", l=P)
        st = sb("st", [P, 6])
        mv = sb("mv", [P, 2])
        vstd = sb("vstd", [P, 2])
        runmax = sb("runmax", [P, H + 1])
        chmax = sb("chmax", [P, H])
        chsq = sb("chsq", [P, 2])
        amax = sb("amax", [P, 4])
        gmax = sb("gmax", [P, 4])
        sigma = sb("sigma", [P, 4])
        lnp = sb("lnp", [P, 1])
        den = sb("den", [P, 2 * H])
        O = mrow[:, 0:INNER]
        OT = mrow[:, INNER:2 * INNER].rearrange("p (j l) -> p j l", j=HP)
        qkT = sb("qkT", [P, 4, P])
        va = sb("va", [P, H, VS])
        kv = sb("kv", [P, H, VS])
        qp = P_hi[0][:, :].bitcast(F32), P_hi[1][:, :].bitcast(F32)
        kp = P_lo[0][:, :].bitcast(F32), P_lo[1][:, :].bitcast(F32)
        fneg, fexp = dbuf, pfull
        lg = sb("lg", [P, 8, NE])
        small = sb("small", [P, 8])
        oh = sb("oh", [P, CS])
        comb = dbuf[0]
        disp = dbuf[1]
        dispT = mrow[:, 0:KH * NE * CS].rearrange("p (k n) -> p k n", k=KH)
        combT = mrow[:, 2 * NE * CS:3 * NE * CS].rearrange("p (q s) -> p q s", q=NQ)
        hh = P_hi[0][:, :].bitcast(F32)
        hs = P_hi[1][:, :].bitcast(F32)
        hg = P_lo[0][:, :].bitcast(F32)
        hT = P_lo[1][:, :].bitcast(F32).rearrange("p (t n) -> p t n", t=FT)
        y = sb("y", [P, D])
        res = sb("res", [P, D])

        ids = sem("ids")
        s_x = sem("s_x")
        s_wq = sem("s_wq")
        s_wk = sem("s_wk")
        s_wv = sem("s_wv")
        s_tail = sem("s_tail")
        bd_zero = sem("bd_zero")
        dve = sem("dve")
        act_own = sem("act_own")
        pool_own = sem("pool_own")
        var_ready = sem("var_ready")
        std_ready = sem("std_ready")
        xn_ready = sem("xn_ready")
        xnT_ps = sem("xnT_ps")
        xnT_ready = sem("xnT_ready")
        wkT_ps = sem("wkT_ps")
        wkT_ready = sem("wkT_ready")
        q_ps = sem("q_ps")
        q_ready = sem("q_ready")
        A_even = sem("A_even")
        A_ps = sem("A_ps")
        Ahi_ready = sem("Ahi_ready")
        A_ready = sem("A_ready")
        wvhi_ready = sem("wvhi_ready")
        wv_ready = sem("wv_ready")
        raw_loaded = [sem(f"raw_loaded{b}") for b in range(2)]
        sq_done = sem("sq_done")
        merged = sem("merged")
        tr_ready = sem("tr_ready")
        ctxhi_ready = sem("ctxhi_ready")
        ctxlo_ready = sem("ctxlo_ready")
        spilled = [sem(f"spilled{b}") for b in range(2)]
        smax_ready = sem("smax_ready")
        smax_used = sem("smax_used")
        diag_ready = sem("diag_ready")
        mrow_ps = sem("mrow_ps")
        mrow_ready = sem("mrow_ready")
        wT_ps = sem("wT_ps")
        wT_ready = sem("wT_ready")
        wmax_ready = sem("wmax_ready")
        gmax_ready = sem("gmax_ready")
        sig_ready = sem("sig_ready")
        vone_ready = sem("vone_ready")
        acc_zero = sem("acc_zero")
        cT_loaded = [sem(f"cT_loaded{b}") for b in range(2)]
        v_ready = sem("v_ready")
        vhi_ready = sem("vhi_ready")
        vlo_ready = sem("vlo_ready")
        s_ready = sem("s_ready")
        d_ready = sem("d_ready")
        exp_done = sem("exp_done")
        p_ready = sem("p_ready")
        pv_done = sem("pv_done")
        O_ready = sem("O_ready")
        OT_ps = sem("OT_ps")
        OT_ready = sem("OT_ready")
        xa_ps = sem("xa_ps")
        qkv_ps = sem("qkv_ps")
        qkv_ready = sem("qkv_ready")
        feat_ps = sem("feat_ps")
        neg_ready = sem("neg_ready")
        fexp_ready = sem("fexp_ready")
        feat_ready = sem("feat_ready")
        kv_ps = sem("kv_ps")
        kv_ready = sem("kv_ready")
        at_ps = sem("at_ps")
        at_ready = sem("at_ready")
        atT_ps = sem("atT_ps")
        atT_ready = sem("atT_ready")
        sa_ps = sem("sa_ps")
        lg_ps = sem("lg_ps")
        lmax_ready = sem("lmax_ready")
        lexp_ready = sem("lexp_ready")
        mask_ready = sem("mask_ready")
        rank_ps = sem("rank_ps")
        comb_ready = sem("comb_ready")
        disp_ps = sem("disp_ps")
        disp_ready = sem("disp_ready")
        unit_loaded = [sem(f"unit_loaded{i}") for i in range(UNITS)]
        unit_used = sem("unit_used")
        y_summed = sem("y_summed")
        combT_ready = sem("combT_ready")
        hcopy_ready = sem("hcopy_ready")
        u_ready = sem("u_ready")
        tanh_ready = sem("tanh_ready")
        g_ready = sem("g_ready")
        hT_ps = sem("hT_ps")
        hT_ready = sem("hT_ready")
        y_ready = sem("y_ready")
        out_ps = sem("out_ps")
        res_ready = sem("res_ready")
        stored = sem("stored")

        x2d = x.rearrange("a n d -> (a n) d")
        out2d = out.rearrange("a n d -> (a n) d")
        ctx_chunks = ctx_in.rearrange("a (c j p) k -> (a c) p j k", j=CT, p=P)
        spill_chunks = spill.rearrange("(c j) p n -> c p j n", j=CT)
        order = [(w1, 0)] + [(w, q) for q in range(1, NQ) for w, q in ((w1, q), (w2, q - 1))] + [(w2, NQ - 1)]
        units = [(w, q * QE + j) for w, q in order for j in range(QE)]
        up_done = [QE * ([(w is w1, n) for w, n in order].index((True, q)) + 1) for q in range(NQ)]
        down_done = [QE * ([(w is w1, n) for w, n in order].index((False, q)) + 1) for q in range(NQ)]
        T_LAST = NG * NT

        def skip_first(eng, semaphore, count):
            if not isinstance(count, int) or count > 0:
                eng.wait_ge(semaphore, count)

        def acc_of(h):
            return bk(5 + h // AH)[:, (h % AH) * (DH + 1):(h % AH + 1) * (DH + 1)]

        block = ctx.enter_context(nc.Block())

        @block.sync
        def _(sp):
            sp.dma_start(x_sb[:, :], x2d).then_inc(s_x, 16)
            sp.dma_start(Wk_sb, Wk.rearrange("(k p) n -> p k n", p=P)).then_inc(s_wk, 16)
            sp.dma_start(Wq_sb, Wq.rearrange("(k p) n -> p k n", p=P)).then_inc(s_wq, 16)
            for b in range(2):
                sp.dma_start(raw[b], ctx_chunks[b]).then_inc(raw_loaded[b], 16)
            sp.dma_start(Wv_sb, Wv.rearrange("(k p) n -> p k n", p=P)).then_inc(s_wv, 16)

            def chunk(c, b, load):
                if load:
                    sp.wait_ge(sq_done, c + 1)
                    sp.wait_ge(tr_ready, c * 2 + 2)
                    sp.dma_start(raw[b], ctx_chunks[c + 2]).then_inc(raw_loaded[b], 16)
                sp.wait_ge(ctxlo_ready, c * 2 + 2)
                sp.dma_start(spill_chunks[c], ctxT[b][:, :, :, :, :].rearrange("p j s k r -> p j (s k r)").bitcast(F32)
                             ).then_inc(spilled[b], 16)

            with sp.Fori(0, NC // 2 - 1) as i:
                for b in range(2):
                    chunk(i * 2 + b, b, True)
            for b in range(2):
                chunk(NC - 2 + b, b, False)

            def load_unit(n):
                w, e = units[n]
                dst = unit[n % UNITS][:, :]
                if w is w1:
                    dst, src = dst.rearrange("p (k f) -> p k f", k=KH), w[e].rearrange("(k p) f -> p k f", p=P)
                else:
                    dst, src = dst.rearrange("p (t d) -> p t d", t=FT), w[e].rearrange("(t p) d -> p t d", p=P)
                sp.dma_start(dst, src).then_inc(unit_loaded[n % UNITS], 16)

            for b in range(2):
                sp.wait_ge(spilled[b], 16 * (NC // 2))
            for b in range(2):
                sp.dma_start(cT[b][:, :, :, :].rearrange("p s k r -> p (s k r)").bitcast(F32), spill[b]
                             ).then_inc(cT_loaded[b], 16)
            sp.wait_ge(A_ready, 2 * NG)
            sp.wait_ge(wv_ready, 1)
            sp.wait_ge(sq_done, NC)
            for n in range(UNITS):
                load_unit(n)
            with sp.Fori(0, NT // 2 - 1) as i:
                for b in range(2):
                    sp.wait_ge(s_ready, i * (2 * NG) + NG * (b + 1))
                    sp.dma_start(cT[b][:, :, :, :].rearrange("p s k r -> p (s k r)").bitcast(F32),
                                 spill[i * 2 + (b + 2)]).then_inc(cT_loaded[b], 16)
            for n in range(UNITS, len(units)):
                sp.wait_ge(unit_used, n - UNITS + 1)
                load_unit(n)
            sp.wait_ge(res_ready, 1)
            sp.dma_start(out2d, res[:, :]).then_inc(stored, 16)
            sp.wait_ge(stored, 16)

        @block.gpsimd
        def _(pool):
            pool.memset(ident[:, :], 0.0).then_inc(pool_own, 1)
            pool.memset(ones[:, :], 1.0).then_inc(pool_own, 1)
            pool.memset(bd[:, :, :], 0.0).then_inc(bd_zero, 1)
            pool.wait_ge(pool_own, 2)
            pool.affine_select(out=ident[:, :], in_=ident[:, :], compare_op=ALU.not_equal, fill=1.0,
                               base=0, pattern=[[-1, P]], channel_multiplier=1).then_inc(ids, 1)
            pool.affine_select(out=upper[:, :], in_=ones[:, :], compare_op=ALU.is_ge, fill=0.0,
                               base=0, pattern=[[1, P]], channel_multiplier=-1).then_inc(ids, 1)
            pool.iota(iota_i[:, :], pattern=[[1, CS]], base=0, channel_multiplier=0).then_inc(ids, 1)
            pool.memset(zeros16[:, :], 0.0).then_inc(ids, 1)
            pool.memset(lnp[:, :], LOG_PSCALE).then_inc(ids, 1)
            for b in range(2):
                pool.memset(V_hi[b][:, :, :], 1.0).then_inc(vone_ready, 1)
            pool.memset(va[:, :, :], 1.0).then_inc(vone_ready, 1)
            pool.wait_ge(wmax_ready, 2)
            pool.partition_all_reduce(gmax[:, 0:2], amax[:, 0:2], P, RMAX).then_inc(gmax_ready, 1)

        @block.scalar
        def _(act):
            for r in range(6):
                act.dma_start(Wqkv_sb[r], W_qkv[r * P:(r + 1) * P, :]).then_inc(s_tail, 16)
            for r in range(2):
                act.dma_start(Wout_sb[r], W_out[r * P:(r + 1) * P, :]).then_inc(s_tail, 16)
            act.dma_start(gate_sb, gate_w).then_inc(s_tail, 16)
            act.dma_start(Wo_sb[:, :, :], Wo.rearrange("(j p) d -> p j d", p=P)).then_inc(s_tail, 16)
            act.dma_start(b_sb[:, :], b_out.rearrange("(a d) -> a d", a=1)).then_inc(s_tail, 16)
            act.wait_ge(bd_zero, 1)
            for h in range(H):
                r = h % 8 * HD
                act.dma_start(bd[r:r + HD, h // 8, h % 8 * F:(h % 8 + 1) * F], proj[h]).then_inc(s_tail, 16)

            def root(n):
                act.wait_ge(var_ready, n + 1)
                nc.scalar.activation(vstd[:, 1:2], vstd[:, 0:1], ACT.Sqrt).then_inc(std_ready, 1)

            root(0)
            for g in range(4):
                act.wait_ge(wkT_ps, g + 1)
                nc.scalar.copy(WkT[:, 2 * g:2 * g + 2, :].rearrange("p j k -> p (j k)"), bk(g)).then_inc(wkT_ready, 1)
            for n in range(2 * NG):
                act.wait_ge(A_ps, n + 1)
                nc.scalar.copy(A_hi[:, n // NG, n % NG * BANK:(n % NG + 1) * BANK], bk(n)).then_inc(Ahi_ready, 1)

            def square(c, b, n):
                act.wait_ge(raw_loaded[b], 16 * n)
                skip_first(act, merged, c - 1)
                nc.scalar.activation(P_hi[b][:, 0:CT * D], raw[b].rearrange("p j k -> p (j k)"), ACT.Square,
                                     accum_out=chsq[:, b:b + 1]).then_inc(sq_done, 1)

            def split_hi(c, b, i):
                skip_first(act, smax_ready, (c - 1) * H)
                skip_first(act, spilled[b], i * 16)
                for f, (j0, j1) in enumerate(((0, 4), (4, CT))):
                    act.wait_ge(tr_ready, c * 2 + (f + 1))
                    nc.scalar.copy(ctxT[b][:, j0:j1, 0, :, :].rearrange("p j k r -> p j (k r)"),
                                   bank[2 + f][:, :, :].rearrange("p a n -> p (a n)")[:, 0:(j1 - j0) * D]
                                   .rearrange("p (j n) -> p j n", n=D)).then_inc(ctxhi_ready, 1)

            split_hi(0, 0, 0)
            square(0, 0, 1)
            split_hi(1, 1, 0)
            square(1, 1, 1)
            with act.Fori(1, NC // 2) as i:
                for b in range(2):
                    split_hi(i * 2 + b, b, i)
                    square(i * 2 + b, b, i + 1)

            act.wait_ge(wT_ps, 1)
            for n in range(3):
                nc.scalar.copy(WqkvT[:, :, :].rearrange("p k n -> p (k n)")[:, n * BANK:(n + 1) * BANK],
                               bk(4 + n)).then_inc(wT_ready, 1)
            nc.scalar.copy(WoutT[:, :, :].rearrange("p k n -> p (k n)"), bk(7)).then_inc(wT_ready, 1)
            act.wait_ge(wT_ps, 2)
            nc.scalar.copy(gateT[:, :, :].rearrange("p k n -> p (k n)"), bk(4, KH * NE)).then_inc(wT_ready, 1)
            for g in range(NG):
                act.wait_ge(mrow_ps, g + 1)
                nc.scalar.copy(mrow[:, g * BANK:(g + 1) * BANK], bk(g)).then_inc(mrow_ready, 1)
            act.wait_ge(gmax_ready, 1)
            nc.scalar.activation(sigma[:, 1:2], gmax[:, 0:1], ACT.Sqrt).then_inc(sig_ready, 1)
            act.wait_ge(sig_ready, 2)
            act.wait_ge(vone_ready, 3)
            act.wait_ge(ids, 5)
            act.wait_ge(sq_done, NC)

            def v_high(t, b, half):
                if half == 0:
                    skip_first(act, pv_done, (t - 1) * NG)
                act.wait_ge(v_ready, t * 2 + (half + 1))
                nc.scalar.activation(V_hi[b][:, half * 8:(half + 1) * 8, 0:DH], bk(4).rearrange("p (h d) -> p h d", d=DH),
                                     ACT.Copy, scale=sigma[:, 0:1]).then_inc(vhi_ready, 1)

            def exps(t, b, g):
                if g == 0:
                    skip_first(act, pv_done, (t - 1) * NG)
                act.wait_ge(d_ready, t * NG + (g + 1))
                nc.scalar.activation(P_hi[b][:, g * BANK:(g + 1) * BANK], dbuf[g % 2], ACT.Exp,
                                     bias=lnp[:, 0:1], scale=SCALE).then_inc(act_own, 1)
                skip_first(act, p_ready, t * NG + (g - 1))
                nc.scalar.activation(pfull[g % 2], dbuf[g % 2], ACT.Exp,
                                     bias=lnp[:, 0:1], scale=SCALE).then_inc(exp_done, 1)

            def tile(t, b):
                v_high(t, b, 0)
                exps(t, b, 0)
                exps(t, b, 1)
                v_high(t, b, 1)
                exps(t, b, 2)
                exps(t, b, 3)

            tile(0, 0)
            tile(1, 1)
            with act.Fori(1, NT // 2) as i:
                for b in range(2):
                    tile(i * 2 + b, b)

            for n in range(2):
                act.wait_ge(OT_ps, n + 1)
                nc.scalar.copy(OT[:, 4 * n:4 * n + 4, :].rearrange("p j l -> p (j l)"), bk(n)).then_inc(OT_ready, 1)
            root(1)
            act.wait_ge(qkv_ps, 1)
            nc.scalar.copy(qkT[:, :, :].rearrange("p j n -> p (j n)"), bk(4)).then_inc(qkv_ready, 1)
            for n in range(8):
                act.wait_ge(neg_ready, n + 1)
                nc.scalar.activation(fexp[n % 2], fneg[n % 2], ACT.Exp).then_inc(fexp_ready, 1)
            root(2)
            act.wait_ge(lmax_ready, 1)
            nc.scalar.activation(lg[:, 1, :], lg[:, 0, :], ACT.Exp, bias=small[:, 1:2],
                                 accum_out=small[:, 2:3]).then_inc(lexp_ready, 1)
            for n in range(2):
                act.wait_ge(disp_ps, n + 1)
                nc.scalar.copy(dispT[:, n, :], bk(n)).then_inc(disp_ready, 1)
            act.wait_ge(disp_ps, 3)
            nc.scalar.copy(combT.rearrange("p q s -> p (q s)"), bk(2)).then_inc(combT_ready, 1)

            def hidden(q):
                hp = bank[q % 2][:, :, :].rearrange("p a n -> p (a n)")
                act.wait_ge(unit_used, up_done[q])
                skip_first(act, g_ready, q)
                nc.scalar.mul(hs, hp, 0.5).then_inc(hcopy_ready, 1)
                nc.scalar.activation(hg, hp, ACT.Square).then_inc(hcopy_ready, 1)
                act.wait_ge(u_ready, q + 1)
                nc.scalar.activation(hg, hh, ACT.Tanh, scale=2 * GELU_A).then_inc(tanh_ready, 1)

            def hidden_T(q):
                act.wait_ge(hT_ps, q + 1)
                if q > 0:
                    act.wait_ge(unit_used, down_done[q - 1])
                nc.scalar.copy(hT.rearrange("p t n -> p (t n)"), bank[2][:, :, :].rearrange("p a n -> p (a n)")
                               ).then_inc(hT_ready, 1)

            for q in range(NQ):
                hidden(q)
                hidden_T(q)

        @block.vector
        def _(dve_):
            steps = [0]

            def link(ins):
                steps[0] += 1
                ins.then_inc(dve, 1)
                dve_.wait_ge(dve, steps[0])

            v = nc.vector

            def layer_norm(n):
                link(v.bn_stats(st[:, :], x_sb[:, :]))
                link(v.bn_aggr(mv[:, :], st[:, :]))
                v.tensor_scalar(vstd[:, 0:1], mv[:, 1:2], EPS, None, ALU.add).then_inc(var_ready, 1)
                dve_.wait_ge(std_ready, n + 1)
                link(v.reciprocal(vstd[:, 0:1], vstd[:, 1:2]))
                v.tensor_scalar(xn[:, :], x_sb[:, :], mv[:, 0:1], vstd[:, 0:1], ALU.subtract, ALU.mult
                                ).then_inc(xn_ready, 1)

            def take_xnT(n, i):
                dve_.wait_ge(xnT_ps, n + 1)
                v.tensor_copy(xnT[:, :, :].rearrange("p k l -> p (k l)"), bk(i, D)).then_inc(xnT_ready, 1)

            dve_.wait_ge(s_x, 16)
            layer_norm(0)
            take_xnT(0, 7)
            for n in range(2):
                dve_.wait_ge(q_ps, n + 1)
                v.tensor_copy(qT[:, 4 * n:4 * n + 4, :].rearrange("p j l -> p (j l)"), bk(4 + n)).then_inc(q_ready, 1)
            dve_.wait_ge(ids, 3)
            v.tensor_copy(iota_f[:, :], iota_i[:, :])
            link(v.memset(runmax[:, H:H + 1], 0.0))
            link(v.memset(runmax[:, 0:H], -3.0e38))
            for n in range(2 * NG):
                sl = slice(n % NG * BANK, (n % NG + 1) * BANK)
                dve_.wait_ge(Ahi_ready, n + 1)
                v.tensor_tensor(A_lo[:, n // NG, sl], bk(n), A_hi[:, n // NG, sl].bitcast(F32), ALU.subtract
                                ).then_inc(A_ready, 1)

            def split_lo(c, b, f):
                j0, j1 = ((0, 4), (4, CT))[f]
                dve_.wait_ge(ctxhi_ready, c * 2 + (f + 1))
                v.tensor_tensor(ctxT[b][:, j0:j1, 1, :, :].rearrange("p j k r -> p j (k r)"),
                                bank[2 + f][:, :, :].rearrange("p a n -> p (a n)")[:, 0:(j1 - j0) * D]
                                .rearrange("p (j n) -> p j n", n=D),
                                ctxT[b][:, j0:j1, 0, :, :].rearrange("p j k r -> p j (k r)").bitcast(F32),
                                ALU.subtract).then_inc(ctxlo_ready, 1)

            split_lo(0, 0, 0)
            split_lo(0, 0, 1)
            dve_.wait_ge(s_wv, 16)
            link(v.tensor_copy(Wv_hi[:, :, :], Wv_sb))
            v.tensor_tensor(Wv_lo[:, :, :], Wv_sb, Wv_hi[:, :, :].bitcast(F32), ALU.subtract).then_inc(wv_ready, 1)
            v.tensor_reduce(amax[:, 1:2], Wv_sb.rearrange("p k n -> p (k n)"), AX_X, ALU.max,
                            apply_absolute_value=True).then_inc(wmax_ready, 1)

            def maxima(c, b, ahead):
                for h in range(H):
                    dve_.wait_ge(smax_ready, c * H + (h + 1))
                    v.tensor_reduce(chmax[:, h:h + 1], bank[h % 2][:, :, :].rearrange("p a n -> p (a n)")[:, 0:CT * P],
                                    AX_X, ALU.max).then_inc(smax_used, 1)
                    if ahead and h in (3, 8):
                        split_lo(c + 1, 1 - b, (3, 8).index(h))
                dve_.wait_ge(smax_used, (c + 1) * H)
                v.tensor_tensor(runmax[:, 0:H], runmax[:, 0:H], chmax[:, :], ALU.max)
                dve_.wait_ge(sq_done, c + 1)
                v.tensor_tensor(runmax[:, H:H + 1], runmax[:, H:H + 1], chsq[:, b:b + 1], ALU.max
                                ).then_inc(merged, 1)
                dve_.wait_ge(merged, c + 1)

            with dve_.Fori(0, NC // 2 - 1) as i:
                for b in range(2):
                    maxima(i * 2 + b, b, True)
            maxima(NC - 2, 0, True)
            maxima(NC - 1, 1, False)
            v.tensor_copy(amax[:, 0:1], runmax[:, H:H + 1]).then_inc(wmax_ready, 1)
            for g in range(NG):
                skip_first(dve_, mrow_ps, g - 1)
                for j in range(GH):
                    h = g * GH + j
                    last = v.tensor_scalar(dbuf[g % 2][:, j * P:(j + 1) * P], ident[:, :], runmax[:, h:h + 1],
                                           None, ALU.mult)
                last.then_inc(diag_ready, 1)
            dve_.wait_ge(sig_ready, 1)
            link(v.tensor_tensor(sigma[:, 2:3], sigma[:, 1:2], gmax[:, 1:2], ALU.mult))
            link(v.tensor_scalar(sigma[:, 2:3], sigma[:, 2:3], 1e-30, None, ALU.max))
            link(v.reciprocal(sigma[:, 3:4], sigma[:, 2:3]))
            link(v.tensor_scalar(sigma[:, 3:4], sigma[:, 3:4], 2048.0, None, ALU.mult))
            v.tensor_scalar(sigma[:, 0:1].bitcast(I32), sigma[:, 3:4].bitcast(I32), 0x7F800000, None,
                            ALU.bitwise_and).then_inc(sig_ready, 1)
            dve_.wait_ge(sig_ready, 2)
            dve_.wait_ge(mrow_ready, NG)

            def v_low(t, b, half):
                dve_.wait_ge(vhi_ready, t * 2 + (half + 1))
                hs8 = slice(half * 8, (half + 1) * 8)
                v.scalar_tensor_tensor(V_lo[b][:, hs8, 0:DH], bk(4).rearrange("p (h d) -> p h d", d=DH),
                                       sigma[:, 0:1], V_hi[b][:, hs8, 0:DH], ALU.mult, ALU.subtract
                                       ).then_inc(vlo_ready, 1)

            def less_max(t, g):
                skip_first(dve_, exp_done, t * NG + (g - 1))
                dve_.wait_ge(s_ready, t * NG + (g + 1))
                v.tensor_tensor(dbuf[g % 2], bk(g), mrow[:, g * BANK:(g + 1) * BANK], ALU.subtract
                                ).then_inc(d_ready, 1)

            def p_low(t, b, g):
                dve_.wait_ge(exp_done, t * NG + (g + 1))
                v.tensor_tensor(P_lo[b][:, g * BANK:(g + 1) * BANK], pfull[g % 2],
                                P_hi[b][:, g * BANK:(g + 1) * BANK], ALU.subtract).then_inc(p_ready, 1)

            def tile(t, b, first):
                v_low(t, b, 0)
                less_max(t, 0)
                if not first:
                    p_low(t - 1, 1 - b, 3)
                less_max(t, 1)
                p_low(t, b, 0)
                v_low(t, b, 1)
                less_max(t, 2)
                p_low(t, b, 1)
                less_max(t, 3)
                p_low(t, b, 2)

            tile(0, 0, True)
            tile(1, 1, False)
            with dve_.Fori(1, NT // 2) as i:
                for b in range(2):
                    tile(i * 2 + b, b, False)
            p_low(NT - 1, 1, 3)

            dve_.wait_ge(pv_done, T_LAST)
            for n, h0 in enumerate(range(0, H, AH)):
                nh = min(AH, H - h0)
                sums = bk(5 + n, nh * (DH + 1)).rearrange("p (h d) -> p h d", d=DH + 1)[:, :, DH]
                ins = v.tensor_scalar(den[:, h0:h0 + nh], sums, sigma[:, 0:1], None, ALU.mult)
            link(ins)
            link(v.reciprocal(den[:, H:2 * H], den[:, 0:H]))
            for h in range(H):
                ins = v.tensor_scalar(O[:, h * DH:(h + 1) * DH], acc_of(h)[:, 0:DH], den[:, H + h:H + h + 1],
                                      None, ALU.mult)
                if h % 8 == 7:
                    ins.then_inc(O_ready, 1)
            dve_.wait_ge(xa_ps, 1)
            link(v.tensor_tensor(x_sb[:, :], x_sb[:, :], bk(2, D), ALU.add))

            layer_norm(1)
            take_xnT(1, 3)
            dve_.wait_ge(qkv_ps, 2)
            v.tensor_copy(va[:, :, 0:HD], bk(5, D).rearrange("p (h d) -> p h d", d=HD)).then_inc(qkv_ready, 1)

            def negative(n):
                skip_first(dve_, fexp_ready, n - 1)
                dve_.wait_ge(feat_ps, n + 1)
                v.tensor_scalar(fneg[n % 2], bk(n), 0.0, None, ALU.min).then_inc(neg_ready, 1)

            def feature(n):
                dst = (kp, qp)[n // 4][n % 4 // 2][:, n % 2 * BANK:(n % 2 + 1) * BANK]
                dve_.wait_ge(fexp_ready, n + 1)
                v.scalar_tensor_tensor(dst, bk(n), 0.0, fexp[n % 2], ALU.max, ALU.add).then_inc(feat_ready, 1)

            negative(0)
            for n in range(8):
                if n < 7:
                    negative(n + 1)
                feature(n)
            dve_.wait_ge(kv_ps, 1)
            v.tensor_copy(kv[:, :, 0:HD + 1], bk(0, H * (HD + 1)).rearrange("p (h d) -> p h d", d=HD + 1)
                          ).then_inc(kv_ready, 1)
            dve_.wait_ge(at_ps, 1)
            atp = bk(1, H * (HD + 1)).rearrange("p (h d) -> p h d", d=HD + 1)
            link(v.tensor_scalar(den[:, 0:H], atp[:, :, HD], 1e-8, None, ALU.add))
            link(v.reciprocal(den[:, H:2 * H], den[:, 0:H]))
            v.tensor_tensor(xn[:, :].rearrange("p (h d) -> p h d", d=HD), atp[:, :, 0:HD],
                            den[:, H:2 * H].unsqueeze(2).broadcast_to([P, H, HD]), ALU.mult).then_inc(at_ready, 1)
            dve_.wait_ge(atT_ps, 1)
            v.tensor_copy(xnT[:, :, :].rearrange("p k l -> p (k l)"), bk(2, D)).then_inc(atT_ready, 1)
            dve_.wait_ge(sa_ps, 1)
            link(v.tensor_tensor(x_sb[:, :], x_sb[:, :], bk(3, D), ALU.add))

            layer_norm(2)
            take_xnT(2, 4)
            dve_.wait_ge(lg_ps, 1)
            link(v.tensor_copy(lg[:, 0, :], bk(5, NE)))
            link(v.tensor_reduce(small[:, 0:1], lg[:, 0, :], AX_X, ALU.max))
            v.tensor_scalar(small[:, 1:2], small[:, 0:1], -1.0, None, ALU.mult).then_inc(lmax_ready, 1)
            link(v.tensor_scalar(lg[:, 2, :], lg[:, 0, :], small[:, 0:1], None, ALU.is_ge))
            link(v.scalar_tensor_tensor(lg[:, 3, :], lg[:, 2, :], -64.0, iota_f[:, 0:NE], ALU.mult, ALU.add))
            link(v.tensor_reduce(small[:, 4:5], lg[:, 3, :], AX_X, ALU.min))
            v.tensor_scalar(lg[:, 4, :], lg[:, 3, :], small[:, 4:5], None, ALU.is_equal).then_inc(mask_ready, 1)
            dve_.wait_ge(lexp_ready, 1)
            link(v.reciprocal(small[:, 3:4], small[:, 2:3]))
            link(v.tensor_scalar(lg[:, 1, :], lg[:, 1, :], small[:, 3:4], None, ALU.mult))
            dve_.wait_ge(rank_ps, 1)
            link(v.scalar_tensor_tensor(lg[:, 4, :], bk(6, NE), CAP + 0.5, lg[:, 4, :], ALU.is_lt, ALU.mult))
            link(v.scalar_tensor_tensor(lg[:, 5, :], bk(6, NE), -1.0, lg[:, 4, :], ALU.add, ALU.mult))
            link(v.tensor_reduce(small[:, 5:6], lg[:, 5, :], AX_X, ALU.add))
            link(v.tensor_tensor(lg[:, 6, :], lg[:, 4, :], lg[:, 1, :], ALU.mult))
            link(v.tensor_scalar(oh[:, :], iota_f[:, :], small[:, 5:6], None, ALU.is_equal))
            link(v.tensor_tensor(comb.rearrange("p (e c) -> p e c", c=CS),
                                 lg[:, 6, :].unsqueeze(2).broadcast_to([P, NE, CS]),
                                 oh[:, :].unsqueeze(1).broadcast_to([P, NE, CS]), ALU.mult))
            v.tensor_scalar(disp, comb, 0.0, None, ALU.is_gt).then_inc(comb_ready, 1)

            def gelu(q):
                dve_.wait_ge(hcopy_ready, 2 * q + 2)
                link(v.tensor_scalar(hg, hg, GELU_B, 1.0, ALU.mult, ALU.add))
                skip_first(dve_, hT_ps, q)
                v.tensor_tensor(hh, hg, hs, ALU.mult).then_inc(u_ready, 1)
                dve_.wait_ge(tanh_ready, q + 1)
                v.scalar_tensor_tensor(hh, hg, 1.0, hs, ALU.add, ALU.mult).then_inc(g_ready, 1)

            def take_y(q):
                skip_first(dve_, y_summed, q)
                dve_.wait_ge(unit_used, down_done[q])
                v.tensor_copy(y[:, :], bk(6, D)).then_inc(y_ready, 1)

            for q in range(NQ):
                gelu(q)
                take_y(q)
            dve_.wait_ge(y_summed, NQ)
            v.tensor_tensor(res[:, :], x_sb[:, :], bk(7, D), ALU.add).then_inc(res_ready, 1)

        @block.tensor
        def _(pe):
            def mm(out_, lhsT, rhs, start=True, stop=True):
                return pe.matmul(out_, lhsT, rhs, start=start, stop=stop, skip_group_check=True)

            pe.wait_ge(ids, 1)
            pe.wait_ge(s_wk, 16)
            for g in range(4):
                for j in range(2 * g, 2 * g + 2):
                    for k in range(KH):
                        ins = pe.transpose(bk(g)[:, (j % 2 * KH + k) * P:(j % 2 * KH + k + 1) * P],
                                           Wk_sb[:, k, j * P:(j + 1) * P], ident[:, :])
                ins.then_inc(wkT_ps, 1)

            def transpose_tokens(n, i):
                pe.wait_ge(xn_ready, n + 1)
                for k in range(KH):
                    ins = pe.transpose(bk(i)[:, k * P:(k + 1) * P], xn[:, k * P:(k + 1) * P], ident[:, :])
                ins.then_inc(xnT_ps, 1)
                pe.wait_ge(xnT_ready, n + 1)

            transpose_tokens(0, 7)
            pe.wait_ge(s_wq, 16)
            for j in range(HP):
                for k in range(KH):
                    ins = mm(bk(4 + j // 4)[:, j % 4 * P:(j % 4 + 1) * P], Wq_sb[:, k, j * P:(j + 1) * P],
                             xnT[:, k, :], k == 0, k == KH - 1)
                if j % 4 == 3:
                    ins.then_inc(q_ps, 1)
            pe.wait_ge(wkT_ready, 4)
            pe.wait_ge(q_ready, 2)
            for r in (0, DH):
                if r:
                    pe.wait_ge(A_even, 1)
                for k in range(KH):
                    for g in range(NG):
                        for h in range(g * GH + r // DH, (g + 1) * GH, 2):
                            ins = mm(bk(k * NG + g)[:, h % GH * P:(h % GH + 1) * P],
                                     WkT[r:r + DH, h // 2, k * P:(k + 1) * P], qT[r:r + DH, h // 2, :])
                        if r:
                            ins.then_inc(A_ps, 1)
                if not r:
                    ins.then_inc(A_even, 1)
            pe.wait_ge(A_ready, 2 * NG)

            def turn(c, b, n):
                pe.wait_ge(raw_loaded[b], 16 * n)
                for f, (j0, j1) in enumerate(((0, 4), (4, CT))):
                    skip_first(pe, ctxlo_ready, c * 2 + (f - 1))
                    for j in range(j0, j1):
                        for k in range(KH):
                            o = (j - j0) * D + k * P
                            ins = pe.transpose(bank[2 + f][:, o // BANK, o % BANK:o % BANK + P],
                                               raw[b][:, j, k * P:(k + 1) * P], ident[:, :])
                    ins.then_inc(tr_ready, 1)

            def prescores(c, b, first):
                pe.wait_ge(ctxhi_ready, c * 2 + 2)
                for h in range(H):
                    if not (first and h < 2):
                        pe.wait_ge(smax_used, c * H + (h - 1))
                    for half, (j0, j1) in enumerate(((0, 4), (4, CT))):
                        for k in range(KH):
                            ins = mm(bank[h % 2][:, half, 0:(j1 - j0) * P], A_hi[:, k, h * P:(h + 1) * P],
                                     ctxT[b][:, j0:j1, 0, k, :], k == 0, k == KH - 1)
                    ins.then_inc(smax_ready, 1)

            turn(0, 0, 1)
            turn(1, 1, 1)
            prescores(0, 0, True)
            turn(2, 0, 2)
            prescores(1, 1, False)
            with pe.Fori(1, NC // 2 - 1) as i:
                turn(i * 2 + 1, 1, i + 1)
                prescores(i * 2, 0, False)
                turn(i * 2 + 2, 0, i + 2)
                prescores(i * 2 + 1, 1, False)
            turn(NC - 1, 1, NC // 2)
            prescores(NC - 2, 0, False)
            prescores(NC - 1, 1, False)

            pe.wait_ge(s_tail, 16 * (11 + H))
            pe.wait_ge(ctxlo_ready, 2 * NC)
            for k in range(KH):
                for r in range(6):
                    n = k * 6 + r
                    pe.transpose(bk(4 + n // 4)[:, n % 4 * P:(n % 4 + 1) * P], Wqkv_sb[r][:, k * P:(k + 1) * P], ident[:, :])
            for k in range(KH):
                for r in range(2):
                    ins = pe.transpose(bk(7)[:, (k * 2 + r) * P:(k * 2 + r + 1) * P],
                                       Wout_sb[r][:, k * P:(k + 1) * P], ident[:, :])
            ins.then_inc(wT_ps, 1)
            pe.wait_ge(wT_ready, 1)
            for k in range(KH):
                ins = pe.transpose(bk(4)[:, k * NE:(k + 1) * NE], gate_sb[:, k * P:(k + 1) * P], ident[0:NE, 0:NE])
            ins.then_inc(wT_ps, 1)
            pe.wait_ge(smax_used, NC * H)
            for g in range(NG):
                pe.wait_ge(diag_ready, g + 1)
                mm(bk(g), ones[:, :], dbuf[g % 2]).then_inc(mrow_ps, 1)
            pe.wait_ge(wT_ready, 5)
            pe.wait_ge(ids, 5)
            for n in range(3):
                mm(bk(5 + n), zeros16[:, 0:P], zeros16[:, :], True, False)
            pe.wait_ge(mrow_ready, NG)
            pe.wait_ge(wv_ready, 1)

            PARTS = ((0, 0), (0, 1), (1, 0))

            def values(t, half):
                skip_first(pe, vlo_ready, t * 2 + half)
                n = 0
                for s, w in PARTS:
                    for k in range(KH):
                        ins = mm(bk(4), cTt[s][k], (Wv_hi, Wv_lo)[w][:, k, half * BANK:(half + 1) * BANK],
                                 n == 0, n == 5)
                        n += 1
                ins.then_inc(v_ready, 1)

            def scores(t, g):
                skip_first(pe, d_ready, (t - 1) * NG + (g + 1))
                n = 0
                for s, w in PARTS:
                    for k in range(KH):
                        ins = mm(bk(g), cTt[s][k], (A_hi, A_lo)[w][:, k, g * BANK:(g + 1) * BANK], n == 0, n == 5)
                        n += 1
                ins.then_inc(s_ready, 1)

            def weigh(t, b, g):
                pe.wait_ge(p_ready, t * NG + (g + 1))
                if g == 0:
                    pe.wait_ge(vlo_ready, t * 2 + 2)
                for h in range(g * GH, (g + 1) * GH):
                    hi, lo = P_hi[b][:, h * P:(h + 1) * P], P_lo[b][:, h * P:(h + 1) * P]
                    mm(acc_of(h), hi, V_hi[b][:, h, 0:DH + 1], False, False)
                    mm(acc_of(h)[:, 0:DH], hi, V_lo[b][:, h, 0:DH], False, False)
                    ins = mm(acc_of(h), lo, V_hi[b][:, h, 0:DH + 1], False, False)
                ins.then_inc(pv_done, 1)

            def tile(t, b, n, first):
                pe.wait_ge(cT_loaded[b], 16 * n)
                cTt[:] = [[cT[b][:, s, k, :] for k in range(KH)] for s in range(2)]
                values(t, 0)
                for g in range(NG):
                    if g == 2:
                        values(t, 1)
                    scores(t, g)
                    if not first:
                        weigh(t - 1, 1 - b, g)

            cTt = []
            tile(0, 0, 1, True)
            tile(1, 1, 1, False)
            with pe.Fori(1, NT // 2) as i:
                for b in range(2):
                    tile(i * 2 + b, b, i + 1, False)
            for g in range(NG):
                weigh(NT - 1, 1, g)

            for j in range(HP):
                if j % 4 == 0:
                    pe.wait_ge(O_ready, j // 4 + 1)
                ins = pe.transpose(bk(j // 4)[:, j % 4 * P:(j % 4 + 1) * P], O[:, j * P:(j + 1) * P], ident[:, :])
                if j % 4 == 3:
                    ins.then_inc(OT_ps, 1)
            for j in range(HP):
                if j % 4 == 0:
                    pe.wait_ge(OT_ready, j // 4 + 1)
                ins = mm(bk(2, D), OT[:, j, :], Wo_sb[:, j, :], j == 0, j == HP - 1)
            ins.then_inc(xa_ps, 1)

            transpose_tokens(1, 3)
            for j in range(4):
                for k in range(KH):
                    ins = mm(bk(4)[:, j * P:(j + 1) * P], WqkvT[:, k, j * P:(j + 1) * P], xnT[:, k, :], k == 0, k == KH - 1)
            ins.then_inc(qkv_ps, 1)
            for k in range(KH):
                ins = mm(bk(5, D), xnT[:, k, :], WqkvT[:, k, 2 * D:3 * D], k == 0, k == KH - 1)
            ins.then_inc(qkv_ps, 1)
            pe.wait_ge(qkv_ready, 2)
            for n in range(4):
                mm(bk(n), qkT[:, 2 + n // 2, :], bd[:, n // 2, n % 2 * BANK:(n % 2 + 1) * BANK]).then_inc(feat_ps, 1)
            for n in range(4):
                for h in range(4 * n, 4 * n + 4):
                    ins = mm(bk(4 + n)[:, h % 4 * P:(h % 4 + 1) * P], bd[:, h // 8, h % 8 * F:(h % 8 + 1) * F],
                             qkT[:, h // 8, :])
                ins.then_inc(feat_ps, 1)
            pe.wait_ge(feat_ready, 4)
            for h in range(H):
                ins = mm(bk(0)[:, h * (HD + 1):(h + 1) * (HD + 1)], kp[h // 8][:, h % 8 * F:(h % 8 + 1) * F],
                         va[:, h, 0:HD + 1])
            ins.then_inc(kv_ps, 1)
            pe.wait_ge(feat_ready, 8)
            pe.wait_ge(kv_ready, 1)
            for h in range(H):
                ins = mm(bk(1)[:, h * (HD + 1):(h + 1) * (HD + 1)], qp[h // 8][:, h % 8 * P:(h % 8 + 1) * P],
                         kv[:, h, 0:HD + 1])
            ins.then_inc(at_ps, 1)
            pe.wait_ge(at_ready, 1)
            for k in range(KH):
                ins = pe.transpose(bk(2)[:, k * P:(k + 1) * P], xn[:, k * P:(k + 1) * P], ident[:, :])
            ins.then_inc(atT_ps, 1)
            pe.wait_ge(atT_ready, 1)
            for k in range(KH):
                mm(bk(3, D), xnT[:, k, :], WoutT[:, k, :], k == 0, False)
            mm(bk(3, D), ones[0:1, :], b_sb[:, :], False, True).then_inc(sa_ps, 1)

            transpose_tokens(2, 4)
            for k in range(KH):
                ins = mm(bk(5, NE), xnT[:, k, :], gateT[:, k, :], k == 0, k == KH - 1)
            ins.then_inc(lg_ps, 1)
            pe.wait_ge(mask_ready, 1)
            mm(bk(6, NE), upper[:, :], lg[:, 4, :]).then_inc(rank_ps, 1)
            pe.wait_ge(comb_ready, 1)
            for k in range(KH):
                mm(bk(k), xn[:, k * P:(k + 1) * P], disp).then_inc(disp_ps, 1)
            for q in range(NQ):
                ins = pe.transpose(bk(2)[:, q * P:(q + 1) * P], comb[:, q * P:(q + 1) * P], ident[:, :])
            ins.then_inc(disp_ps, 1)
            pe.wait_ge(disp_ready, 2)
            pe.wait_ge(combT_ready, 1)

            done = [0]

            def next_unit():
                n = done[0]
                done[0] += 1
                pe.wait_ge(unit_loaded[n % UNITS], 16 * (n // UNITS + 1))
                return unit[n % UNITS][:, :]

            def up(q):
                skip_first(pe, hcopy_ready, 2 * (q - 1))
                for j in range(QE):
                    w = next_unit().rearrange("p (k f) -> p k f", k=KH)
                    c0 = (q * QE + j) * CS
                    for half in range(2):
                        for k in range(KH):
                            ins = mm(bank[q % 2][j * CS:(j + 1) * CS, half, :], dispT[:, k, c0:c0 + CS],
                                     w[:, k, half * BANK:(half + 1) * BANK], k == 0, k == KH - 1)
                    ins.then_inc(unit_used, 1)

            def turn_hidden(q):
                pe.wait_ge(g_ready, q + 1)
                skip_first(pe, hT_ready, q)
                for t in range(FT):
                    ins = pe.transpose(bank[2][:, t // 4, t % 4 * P:(t % 4 + 1) * P], hh[:, t * P:(t + 1) * P], ident[:, :])
                ins.then_inc(hT_ps, 1)

            def down(q):
                pe.wait_ge(hT_ready, q + 1)
                skip_first(pe, y_ready, q)
                for j in range(QE):
                    w = next_unit().rearrange("p (t d) -> p t d", t=FT)
                    for t in range(FT):
                        ins = mm(bk(6)[j * CS:(j + 1) * CS, 0:D], hT[:, t, j * CS:(j + 1) * CS], w[:, t, :],
                                 t == 0, t == FT - 1)
                    ins.then_inc(unit_used, 1)

            def combine(q):
                pe.wait_ge(y_ready, q + 1)
                mm(bk(7, D), combT[:, q, :], y[:, :], q == 0, q == NQ - 1).then_inc(y_summed, 1)

            up(0)
            for q in range(NQ):
                if q + 1 < NQ:
                    up(q + 1)
                turn_hidden(q)
                if q > 0:
                    combine(q - 1)
                down(q)
            combine(NQ - 1)


_INS = ["x", "ctx_1024", "L0_xattn_Wq", "L0_xattn_Wk", "L0_xattn_Wv", "L0_xattn_Wo", "L0_attn_W_qkv",
        "L0_attn_proj", "L0_attn_W_out", "L0_attn_b_out", "L0_ffn_gate_w", "L0_ffn_w1", "L0_ffn_w2"]
_OUTS = [((1, 128, 256), "float32")]


def kernel(**inputs):
    import numpy as _np
    import concourse.bacc as _bacc
    from concourse import mybir as _mybir
    from concourse.bass_utils import run_bass_kernel_spmd as _run

    nc = _bacc.Bacc("TRN2", target_bir_lowering=False, num_devices=1)
    arrays, args = {}, []
    for name in _INS:
        a = _np.ascontiguousarray(inputs[name])
        arrays[f"in_{name}_dram"] = a
        args.append(nc.dram_tensor(f"in_{name}_dram", a.shape, _mybir.dt.from_np(a.dtype), kind="ExternalInput").ap())
    for i, (shape, dtype) in enumerate(_OUTS):
        dt = _mybir.dt.from_np(_np.dtype(dtype))
        args.append(nc.dram_tensor(f"out_{i}_dram", shape, dt, kind="ExternalOutput").ap())
    perceiver_layer(nc, *args)
    r = _run(nc, [arrays], core_ids=[0])
    got = tuple(r.results[0][f"out_{i}_dram"] for i in range(len(_OUTS)))
    return got[0]
```

```python
from contextlib import ExitStack

import concourse.bass as bass
from concourse import mybir

ALU = mybir.AluOpType
ACT = mybir.ActivationFunctionType
AX_X = mybir.AxisListType.X
F32 = mybir.dt.float32
F32R = mybir.dt.float32r
F16 = mybir.dt.float16
I32 = mybir.dt.int32
RMAX = bass.bass_isa.ReduceOp.max

P = 128
D = 256
KH = D // P
H = 16
DH = 64
INNER = H * DH
HP = H // 2
HD = D // H
F = 128
BANK = 512
GH = BANK // P
NG = H // GH
CT = 7
PAIRS = (CT + 1) // 2
STEPS = CT * 4
RING = 2 * CT
LESS = 12
EXP = 13
LOW = 14
WEIGH = 16
TURN = 8
MAX = 9
DIAG = 11
ROW = 11
SUM = 24
SQ = 4
SQ_STEP = 9
SQ_SUM = 18
RHO_STEP = 10
SIG_OWN = 7
PR = 7
VW = DH + 2
AH = 7
VS = HD + 2
NE = 16
FF = 1024
FT = FF // P
CAP = 10
CS = 32
QE = P // CS
NQ = NE // QE
LOG_PSCALE = 11 * 0.6931471805599453
SCALE = DH ** -0.5
EPS = 1e-5
GELU_A = 0.7978845608028654
GELU_B = 0.044715
LATE_UNITS = 8


def perceiver_layer(nc, x, ctx_in, Wq, Wk, Wv, Wo, W_qkv, proj, W_out, b_out, gate_w, w1, w2, out):
    R = ctx_in.shape[1]
    NT = R // P
    NC = NT // CT
    assert R % (P * CT) == 0 and NC % 2 == 0 and NT % 2 == 0 and x.shape[1] == P
    assert CAP == max(int(1.25 * P / NE) + int(1.25 * P / NE) % 2, 4)

    with ExitStack() as ctx:
        def sb(name, shape, dt=F32):
            return ctx.enter_context(nc.sbuf_tensor(name, shape, dt))

        def sem(name):
            return ctx.enter_context(nc.semaphore(name))

        bank = [ctx.enter_context(nc.psum_tensor(f"pair{i}", [P, 2, BANK], F32)) for i in range(4)]

        def bk(i, n=BANK):
            return bank[i // 2][:, i % 2, 0:n]

        with ExitStack() as over:
            def operand(name, shape):
                return over.enter_context(nc.sbuf_tensor(name, shape, F32R))

            A_hi = operand("A_hi", [P, KH, H * P])
            A_lo = operand("A_lo", [P, KH, H * P])
            Wv_hi = operand("Wv_hi", [P, KH, INNER])
            Wv_lo = operand("Wv_lo", [P, KH, INNER])
            ctxT = operand("ctxT", [P, CT, 2, KH, P])
        EARLY_UNITS = (2 * KH * H * P + 2 * KH * INNER + CT * 2 * D) // (KH * FF)
        early = sb("early", [P, 2 * KH * H * P + 2 * KH * INNER + CT * 2 * D])
        ident = sb("ident", [P, P])
        upper = sb("upper", [P, P])
        ones = sb("ones", [P, P])
        ones_r = sb("ones_r", [P, P], F32R)
        iota_i = sb("iota_i", [P, CS], I32)
        iota_f = sb("iota_f", [P, CS])
        diag = sb("diag", [P, GH, P], F32R)
        mnew = sb("mnew", [P, H], F32R)
        Vall = sb("Vall", [P, CT * 2 * H * VW], F16)
        V_hi, V_lo = [Vall[:, :].rearrange("p (s j h d) -> p s j h d", s=2, j=CT, h=H)[:, n] for n in range(2)]
        Pall = sb("Pall", [P, 2 * PR * BANK], F16)
        P_hi, P_lo = [Pall[:, :].rearrange("p (s r n) -> p s r n", s=2, r=PR)[:, n] for n in range(2)]
        Oacc = sb("Oacc", [P, H, VW])
        pool_ = sb("pool_", [P, LATE_UNITS * KH * FF])
        unit = [early[:, n * KH * FF:(n + 1) * KH * FF] for n in range(EARLY_UNITS)]
        unit += [pool_[:, n * KH * FF:(n + 1) * KH * FF] for n in range(LATE_UNITS)]
        UNITS = len(unit)
        place = [0]

        def part(n, at=None):
            at = place[0] if at is None else at
            place[0] = at + n
            return pool_[:, at:at + n]

        ring = part(RING * BANK).rearrange("p (r n) -> p r n", n=BANK)
        dbuf = [part(BANK) for n in range(2)]
        pfull = [part(BANK) for n in range(2)]
        tops = [part(BANK) for n in range(2)]
        mrow = [part(BANK) for n in range(2)]
        raw = part(CT * D).rearrange("p (j k) -> p j k", j=CT)
        qT = part(HP * P).rearrange("p (j l) -> p j l", l=P)
        Wqkv_sb = [part(D) for r in range(6)]
        Wout_sb = [part(D) for r in range(2)]
        gate_sb = part(D)[0:NE]
        assert place[0] <= LATE_UNITS * KH * FF
        Wq_sb = part(KH * INNER, 0).rearrange("p (k n) -> p k n", k=KH)
        Wk_sb = part(KH * INNER).rearrange("p (k n) -> p k n", k=KH)
        WkT = part(KH * INNER).rearrange("p (j k) -> p j k", j=HP)
        Wv_sb = part(KH * INNER).rearrange("p (k n) -> p k n", k=KH)
        Vf = Vall[:, :].bitcast(F32)
        Pf = Pall[:, :].bitcast(F32)
        Wo_sb = sb("Wo_sb", [P, HP, D])
        WqkvT = sb("WqkvT", [P, KH, 3 * D])
        WoutT = sb("WoutT", [P, KH, D])
        gateT = sb("gateT", [P, KH, NE])
        bd = sb("bd", [P, KH, 8 * F])
        b_sb = sb("b_sb", [1, D])
        x_sb = sb("x_sb", [P, D])
        xn = sb("xn", [P, D])
        xnT = sb("xnT", [P, KH, P])
        st = sb("st", [P, 6])
        mv = sb("mv", [P, 2])
        vstd = sb("vstd", [P, 2])
        mold = sb("mold", [P, H])
        blkmax = sb("blkmax", [P, H])
        fall = sb("fall", [P, H])
        alpha = sb("alpha", [P, H])
        squares = sb("squares", [P, CT * D // SQ])
        chsq = sb("chsq", [P, SQ])
        amax = sb("amax", [P, 1])
        wmax = sb("wmax", [P, 2])
        bound = sb("bound", [P, 4])
        sigma = sb("sigma", [P, 1])
        sigma_inv = sb("sigma_inv", [P, 1])
        rho = sb("rho", [P, 1])
        lnp = sb("lnp", [P, 1])
        den = Pf[:, 5 * BANK + 8 * NE:5 * BANK + 8 * NE + 2 * H]
        O = Vf[:, 0:INNER]
        OT = Vf[:, INNER:2 * INNER].rearrange("p (j l) -> p j l", j=HP)
        free = 2 * INNER
        qkT = Vf[:, free + 4096:free + 4096 + 4 * P].rearrange("p (j l) -> p j l", j=4)
        va = Vf[:, free + 4608 + H * VS:free + 4608 + 2 * H * VS].rearrange("p (h d) -> p h d", h=H)
        kv = Vf[:, free + 4608:free + 4608 + H * VS].rearrange("p (h d) -> p h d", h=H)
        qp = Vf[:, free:free + 1024], Vf[:, free + 1024:free + 2048]
        kp = Vf[:, free + 2048:free + 3072], Vf[:, free + 3072:free + 4096]
        fneg = Pf[:, 0:BANK], Pf[:, BANK:2 * BANK]
        fexp = Pf[:, 2 * BANK:3 * BANK], Pf[:, 3 * BANK:4 * BANK]
        lg = Pf[:, 5 * BANK:5 * BANK + 8 * NE].rearrange("p (r e) -> p r e", r=8)
        small = sb("small", [P, 8])
        oh = Pf[:, 6 * BANK:6 * BANK + CS]
        of = Oacc[:, :, :].rearrange("p h d -> p (h d)")
        comb = of[:, 0:NE * CS]
        disp = of[:, NE * CS:2 * NE * CS]
        dispT = O.rearrange("p (k n) -> p k n", k=KH)
        combT = Vf[:, INNER:INNER + NE * CS].rearrange("p (q s) -> p q s", q=NQ)
        hh, hs = qp
        hg = kp[0]
        hT = kp[1].rearrange("p (t n) -> p t n", t=FT)
        y = Pf[:, 4 * BANK:4 * BANK + D]
        res = Pf[:, 4 * BANK + D:4 * BANK + 2 * D]

        ids = sem("ids")
        s_x = sem("s_x")
        s_wq = sem("s_wq")
        s_wk = sem("s_wk")
        s_wv = sem("s_wv")
        s_tail = sem("s_tail")
        bd_zero = sem("bd_zero")
        dve = sem("dve")
        act_own = sem("act_own")
        pool_own = sem("pool_own")
        var_ready = sem("var_ready")
        std_ready = sem("std_ready")
        xn_ready = sem("xn_ready")
        xnT_ps = sem("xnT_ps")
        xnT_ready = sem("xnT_ready")
        wkT_ps = sem("wkT_ps")
        wkT_ready = sem("wkT_ready")
        q_ps = sem("q_ps")
        q_ready = sem("q_ready")
        A_even = sem("A_even")
        A_ps = sem("A_ps")
        Ahi_ready = sem("Ahi_ready")
        A_ready = sem("A_ready")
        wvhi_ready = sem("wvhi_ready")
        wv_ready = sem("wv_ready")
        raw_loaded = sem("raw_loaded")
        sq_done = sem("sq_done")
        sq_ps = sem("sq_ps")
        sig_own = sem("sig_own")
        rho_ready = sem("rho_ready")
        inv_ready = sem("inv_ready")
        tr_ready = sem("tr_ready")
        ctxhi_ready = sem("ctxhi_ready")
        ctxlo_ready = sem("ctxlo_ready")
        copied = sem("copied")
        topped = sem("topped")
        turned = sem("turned")
        blkmax_ready = sem("blkmax_ready")
        mnew_ready = sem("mnew_ready")
        fall_ready = sem("fall_ready")
        diag_ready = sem("diag_ready")
        mold_ready = sem("mold_ready")
        alpha_ready = sem("alpha_ready")
        mrow_ps = sem("mrow_ps")
        mrow_ready = sem("mrow_ready")
        summed = sem("summed")
        shrunk = sem("shrunk")
        wT_ps = sem("wT_ps")
        wT_ready = sem("wT_ready")
        wmax_ready = sem("wmax_ready")
        gmax_ready = sem("gmax_ready")
        sig_ready = sem("sig_ready")
        vone_ready = sem("vone_ready")
        v_ready = sem("v_ready")
        vhi_ready = sem("vhi_ready")
        vlo_ready = sem("vlo_ready")
        s_ready = sem("s_ready")
        d_ready = sem("d_ready")
        exp_done = sem("exp_done")
        p_ready = sem("p_ready")
        pv_done = sem("pv_done")
        O_ready = sem("O_ready")
        OT_ps = sem("OT_ps")
        OT_ready = sem("OT_ready")
        xa_ps = sem("xa_ps")
        qkv_ps = sem("qkv_ps")
        qkv_ready = sem("qkv_ready")
        feat_ps = sem("feat_ps")
        neg_ready = sem("neg_ready")
        fexp_ready = sem("fexp_ready")
        feat_ready = sem("feat_ready")
        kv_ps = sem("kv_ps")
        kv_ready = sem("kv_ready")
        at_ps = sem("at_ps")
        at_ready = sem("at_ready")
        atT_ps = sem("atT_ps")
        atT_ready = sem("atT_ready")
        sa_ps = sem("sa_ps")
        lg_ps = sem("lg_ps")
        lmax_ready = sem("lmax_ready")
        lexp_ready = sem("lexp_ready")
        mask_ready = sem("mask_ready")
        rank_ps = sem("rank_ps")
        comb_ready = sem("comb_ready")
        disp_ps = sem("disp_ps")
        disp_ready = sem("disp_ready")
        unit_loaded = [sem(f"unit_loaded{i}") for i in range(UNITS)]
        unit_used = sem("unit_used")
        y_summed = sem("y_summed")
        combT_ready = sem("combT_ready")
        hcopy_ready = sem("hcopy_ready")
        u_ready = sem("u_ready")
        tanh_ready = sem("tanh_ready")
        g_ready = sem("g_ready")
        hT_ps = sem("hT_ps")
        hT_ready = sem("hT_ready")
        y_ready = sem("y_ready")
        out_ps = sem("out_ps")
        res_ready = sem("res_ready")
        stored = sem("stored")

        x2d = x.rearrange("a n d -> (a n) d")
        out2d = out.rearrange("a n d -> (a n) d")
        ctx_chunks = ctx_in.rearrange("a (c j p) k -> (a c) p j k", j=CT, p=P)
        order = [(w1, 0)] + [(w, q) for q in range(1, NQ) for w, q in ((w1, q), (w2, q - 1))] + [(w2, NQ - 1)]
        units = [(w, q * QE + j) for w, q in order for j in range(QE)]
        up_done = [QE * ([(w is w1, n) for w, n in order].index((True, q)) + 1) for q in range(NQ)]
        down_done = [QE * ([(w is w1, n) for w, n in order].index((False, q)) + 1) for q in range(NQ)]
        T_LAST = NG * NT

        def skip_first(eng, semaphore, count):
            if not isinstance(count, int) or count > 0:
                eng.wait_ge(semaphore, count)

        def acc_of(h):
            return bk(3 + h // GH % 2)[:, h % GH * (DH + 1):(h % GH + 1) * (DH + 1)]

        def tiles_of(p):
            return min(2, CT - 2 * p)

        def pair_at(i, k, lag, first, ahead):
            for p in range(PAIRS):
                t = STEPS - CT + 1 + 3 * p + lag
                if k == t and ahead:
                    return i + 1, p
                if k == t - STEPS and not first:
                    return i, p
            return None

        def values_at(n):
            return bk((2, 7)[n % 2])

        def late(i, k, lag, first, last):
            b = k - lag
            if (first and b < 0) or (last and b >= 0):
                return None
            return i * STEPS + b, b % STEPS

        def late_unit(i, k, lag, first, last):
            b = k - lag
            if b % CT or (first and b < 0) or (last and b >= 0):
                return None
            return i * NG + b // CT, b // CT % NG

        block = ctx.enter_context(nc.Block())

        @block.sync
        def _(sp):
            sp.dma_start(x_sb[:, :], x2d).then_inc(s_x, 16)
            sp.dma_start(Wk_sb, Wk.rearrange("(k p) n -> p k n", p=P)).then_inc(s_wk, 16)
            sp.dma_start(Wq_sb, Wq.rearrange("(k p) n -> p k n", p=P)).then_inc(s_wq, 16)
            sp.dma_start(Wv_sb, Wv.rearrange("(k p) n -> p k n", p=P)).then_inc(s_wv, 16)
            sp.dma_start(raw, ctx_chunks[0]).then_inc(raw_loaded, 16)
            with sp.Fori(0, NC - 1) as i:
                sp.wait_ge(tr_ready, i * PAIRS + PAIRS)
                sp.wait_ge(sq_done, i * SQ + SQ)
                sp.dma_start(raw, ctx_chunks[i + 1]).then_inc(raw_loaded, 16)

            def load_unit(n):
                w, e = units[n]
                dst = unit[n % UNITS]
                if w is w1:
                    dst, src = dst.rearrange("p (k f) -> p k f", k=KH), w[e].rearrange("(k p) f -> p k f", p=P)
                else:
                    dst, src = dst.rearrange("p (t d) -> p t d", t=FT), w[e].rearrange("(t p) d -> p t d", p=P)
                sp.dma_start(dst, src).then_inc(unit_loaded[n % UNITS], 16)

            sp.wait_ge(s_ready, T_LAST)
            sp.wait_ge(v_ready, NC * RING)
            for n in range(EARLY_UNITS):
                load_unit(n)
            sp.wait_ge(p_ready, T_LAST)
            for n in range(EARLY_UNITS, UNITS):
                load_unit(n)
            for n in range(UNITS, len(units)):
                sp.wait_ge(unit_used, n - UNITS + 1)
                load_unit(n)
            sp.wait_ge(res_ready, 1)
            sp.dma_start(out2d, res).then_inc(stored, 16)
            sp.wait_ge(stored, 16)

        @block.gpsimd
        def _(pool):
            pool.memset(ident[:, :], 0.0).then_inc(pool_own, 1)
            pool.memset(ones[:, :], 1.0).then_inc(pool_own, 1)
            pool.memset(bd[:, :, :], 0.0).then_inc(bd_zero, 1)
            pool.wait_ge(pool_own, 2)
            pool.affine_select(out=ident[:, :], in_=ident[:, :], compare_op=ALU.not_equal, fill=1.0,
                               base=0, pattern=[[-1, P]], channel_multiplier=1).then_inc(ids, 1)
            pool.affine_select(out=upper[:, :], in_=ones[:, :], compare_op=ALU.is_ge, fill=0.0,
                               base=0, pattern=[[1, P]], channel_multiplier=-1).then_inc(ids, 1)
            pool.iota(iota_i[:, :], pattern=[[1, CS]], base=0, channel_multiplier=0).then_inc(ids, 1)
            pool.memset(Oacc[:, :, :], 0.0).then_inc(ids, 1)
            pool.memset(lnp[:, :], LOG_PSCALE).then_inc(ids, 1)
            pool.memset(V_hi[:, :, :, DH:DH + 1], 1.0).then_inc(vone_ready, 1)
            pool.wait_ge(wmax_ready, 1)
            pool.partition_all_reduce(wmax[:, 0:1], amax[:, 0:1], P, RMAX).then_inc(gmax_ready, 1)

            def block_(i, first=False):
                for g in range(NG):
                    u = i * NG + g
                    hs4 = slice(g * GH, (g + 1) * GH)
                    pool.wait_ge(mnew_ready, u + 1)
                    pool.tensor_tensor(fall[:, hs4], mold[:, hs4], mnew[:, hs4].bitcast(F32), ALU.subtract
                                       ).then_inc(fall_ready, 1)
                    pool.wait_ge(rho_ready, i + 1)
                    pool.wait_ge(alpha_ready, u + 1)
                    if not first:
                        pool.wait_ge(summed, u + (1 - NG))
                    pool.tensor_tensor(mold[:, hs4], mnew[:, hs4].bitcast(F32), ones[:, 0:GH], ALU.mult
                                       ).then_inc(mold_ready, 1)
                    pool.tensor_tensor(Oacc[:, hs4, DH], Oacc[:, hs4, DH], alpha[:, hs4], ALU.mult)
                    for n in range(GH):
                        h = g * GH + n
                        ins = pool.tensor_scalar(Oacc[:, h, 0:DH], Oacc[:, h, 0:DH], alpha[:, h:h + 1], rho[:, 0:1],
                                                 ALU.mult, ALU.mult)
                    ins.then_inc(shrunk, 1)

            block_(0, first=True)
            with pool.Fori(1, NC) as i:
                block_(i)
            pool.wait_ge(pv_done, T_LAST)
            pool.memset(va, 1.0).then_inc(vone_ready, 1)

        @block.scalar
        def _(act):
            for r in range(6):
                act.dma_start(Wqkv_sb[r], W_qkv[r * P:(r + 1) * P, :]).then_inc(s_tail, 16)
            for r in range(2):
                act.dma_start(Wout_sb[r], W_out[r * P:(r + 1) * P, :]).then_inc(s_tail, 16)
            act.dma_start(gate_sb, gate_w).then_inc(s_tail, 16)
            act.dma_start(Wo_sb[:, :, :], Wo.rearrange("(j p) d -> p j d", p=P)).then_inc(s_tail, 16)
            act.dma_start(b_sb[:, :], b_out.rearrange("(a d) -> a d", a=1)).then_inc(s_tail, 16)
            act.wait_ge(bd_zero, 1)
            for h in range(H):
                r = h % 8 * HD
                act.dma_start(bd[r:r + HD, h // 8, h % 8 * F:(h % 8 + 1) * F], proj[h]).then_inc(s_tail, 16)

            def root(n):
                act.wait_ge(var_ready, n + 1)
                nc.scalar.activation(vstd[:, 1:2], vstd[:, 0:1], ACT.Sqrt).then_inc(std_ready, 1)

            root(0)
            for g in range(4):
                act.wait_ge(wkT_ps, g + 1)
                nc.scalar.copy(WkT[:, 2 * g:2 * g + 2, :].rearrange("p j k -> p (j k)"), bk(g)).then_inc(wkT_ready, 1)
            for n in range(2 * NG):
                act.wait_ge(A_ps, n + 1)
                nc.scalar.copy(A_hi[:, n // NG, n % NG * BANK:(n % NG + 1) * BANK], bk(n)).then_inc(Ahi_ready, 1)

            def split_hi(i, p, first):
                n = tiles_of(p)
                if not first:
                    act.wait_ge(s_ready, i * STEPS + (2 * p + n - CT))
                    act.wait_ge(v_ready, i * RING + (2 * p + n - CT))
                act.wait_ge(tr_ready, i * PAIRS + (p + 1))
                nc.scalar.copy(ctxT[:, 2 * p:2 * p + n, 0, :, :].rearrange("p j k r -> p j (k r)"),
                               bk(5, n * D).rearrange("p (j n) -> p j n", j=n)).then_inc(ctxhi_ready, 1)

            def square(i, n):
                act.wait_ge(raw_loaded, i * 16 + 16)
                if n == 0 and not isinstance(i, int):
                    act.wait_ge(sq_ps, i)
                if not (isinstance(i, int) and i + n == 0):
                    act.wait_ge(sq_done, i * SQ + n)
                src = raw.rearrange("p j k -> p (j k)")[:, n * CT * D // SQ:(n + 1) * CT * D // SQ]
                nc.scalar.activation(squares[:, :], src, ACT.Square, accum_out=chsq[:, n:n + 1]).then_inc(sq_done, 1)

            for n in range(SQ):
                square(0, n)

            act.wait_ge(wT_ps, 1)
            for n in range(3):
                nc.scalar.copy(WqkvT[:, :, :].rearrange("p k n -> p (k n)")[:, n * BANK:(n + 1) * BANK],
                               bk(4 + n)).then_inc(wT_ready, 1)
            nc.scalar.copy(WoutT[:, :, :].rearrange("p k n -> p (k n)"), bk(7)).then_inc(wT_ready, 1)
            act.wait_ge(wT_ps, 2)
            nc.scalar.copy(gateT[:, :, :].rearrange("p k n -> p (k n)"), bk(4, KH * NE)).then_inc(wT_ready, 1)
            for p in range(PAIRS):
                split_hi(0, p, True)
            act.wait_ge(vone_ready, 1)
            act.wait_ge(ids, 5)
            act.wait_ge(wv_ready, 1)
            act.wait_ge(A_ready, 2 * NG)

            def block_(i, first=False, ahead=True, last=False):
                for k in range(STEPS if not last else EXP):
                    pair = None if last else pair_at(i, k, 1, first, ahead)
                    if pair:
                        split_hi(*pair, False)
                    if not last:
                        if not first or k >= RING:
                            act.wait_ge(d_ready, i * STEPS + (k + 1 - RING))
                        act.wait_ge(s_ready, i * STEPS + (k + 1))
                        nc.scalar.copy(ring[:, k % RING, :], bk(k % 2)).then_inc(copied, 1)
                        if k % 2 == 0:
                            half, j = k // RING, k % RING // 2
                            if k == 0:
                                act.wait_ge(sig_ready, i + 1)
                            if not first:
                                act.wait_ge(pv_done, i * STEPS + ((CT, 3 * CT)[half] + j + 1 - STEPS))
                            act.wait_ge(v_ready, i * RING + (k // 2 + 1))
                            nc.scalar.activation(V_hi[:, j, half * 8:half * 8 + 8, 0:DH],
                                                 values_at(k // 2).rearrange("p (h d) -> p h d", d=DH),
                                                 ACT.Copy, scale=sigma[:, :]).then_inc(vhi_ready, 1)
                    if ahead and not last and SQ_STEP <= k < SQ_STEP + 2 * SQ and (k - SQ_STEP) % 2 == 0:
                        square(i + 1, (k - SQ_STEP) // 2)
                    u = late_unit(i, k, ROW, first, last)
                    if u:
                        act.wait_ge(mrow_ps, u[0] + 1)
                        nc.scalar.copy(mrow[u[1] % 2], bk(6)).then_inc(mrow_ready, 1)
                        act.wait_ge(fall_ready, u[0] + 1)
                        hs4 = slice(u[1] * GH, (u[1] + 1) * GH)
                        nc.scalar.activation(alpha[:, hs4], fall[:, hs4], ACT.Exp, scale=SCALE).then_inc(alpha_ready, 1)
                    s = late(i, k, EXP, first, last)
                    if s:
                        if not (first and s[1] < PR):
                            act.wait_ge(pv_done, s[0] + (1 - PR))
                        act.wait_ge(d_ready, s[0] + 1)
                        nc.scalar.activation(P_hi[:, s[1] % PR, :], dbuf[s[1] % 2], ACT.Exp,
                                             bias=lnp[:, 0:1], scale=SCALE).then_inc(act_own, 1)
                        if not (first and s[1] < 2):
                            act.wait_ge(p_ready, s[0] - 1)
                        nc.scalar.activation(pfull[s[1] % 2], dbuf[s[1] % 2], ACT.Exp,
                                             bias=lnp[:, 0:1], scale=SCALE).then_inc(exp_done, 1)

            block_(0, first=True)
            with act.Fori(1, NC - 1) as i:
                block_(i)
            block_(NC - 1, ahead=False)
            block_(NC, last=True)

            for n in range(2):
                act.wait_ge(OT_ps, n + 1)
                nc.scalar.copy(OT[:, 4 * n:4 * n + 4, :].rearrange("p j l -> p (j l)"), bk(n)).then_inc(OT_ready, 1)
            root(1)
            act.wait_ge(qkv_ps, 1)
            nc.scalar.copy(qkT.rearrange("p j n -> p (j n)"), bk(4)).then_inc(qkv_ready, 1)
            for n in range(8):
                act.wait_ge(neg_ready, n + 1)
                nc.scalar.activation(fexp[n % 2], fneg[n % 2], ACT.Exp).then_inc(fexp_ready, 1)
            root(2)
            act.wait_ge(lmax_ready, 1)
            nc.scalar.activation(lg[:, 1, :], lg[:, 0, :], ACT.Exp, bias=small[:, 1:2],
                                 accum_out=small[:, 2:3]).then_inc(lexp_ready, 1)
            for n in range(2):
                act.wait_ge(disp_ps, n + 1)
                nc.scalar.copy(dispT[:, n, :], bk(n)).then_inc(disp_ready, 1)
            act.wait_ge(disp_ps, 3)
            nc.scalar.copy(combT.rearrange("p q s -> p (q s)"), bk(2)).then_inc(combT_ready, 1)

            def hidden(q):
                hp = bank[q % 2][:, :, :].rearrange("p a n -> p (a n)")
                act.wait_ge(unit_used, up_done[q])
                skip_first(act, g_ready, q)
                nc.scalar.mul(hs, hp, 0.5).then_inc(hcopy_ready, 1)
                nc.scalar.activation(hg, hp, ACT.Square).then_inc(hcopy_ready, 1)
                act.wait_ge(u_ready, q + 1)
                nc.scalar.activation(hg, hh, ACT.Tanh, scale=2 * GELU_A).then_inc(tanh_ready, 1)

            def hidden_T(q):
                act.wait_ge(hT_ps, q + 1)
                if q > 0:
                    act.wait_ge(unit_used, down_done[q - 1])
                nc.scalar.copy(hT.rearrange("p t n -> p (t n)"), bank[2][:, :, :].rearrange("p a n -> p (a n)")
                               ).then_inc(hT_ready, 1)

            for q in range(NQ):
                hidden(q)
                hidden_T(q)

        @block.vector
        def _(dve_):
            steps = [0]

            def link(ins):
                steps[0] += 1
                ins.then_inc(dve, 1)
                dve_.wait_ge(dve, steps[0])

            v = nc.vector

            def layer_norm(n):
                link(v.bn_stats(st[:, :], x_sb[:, :]))
                link(v.bn_aggr(mv[:, :], st[:, :]))
                v.tensor_scalar(vstd[:, 0:1], mv[:, 1:2], EPS, None, ALU.add).then_inc(var_ready, 1)
                dve_.wait_ge(std_ready, n + 1)
                link(v.reciprocal(vstd[:, 0:1], vstd[:, 1:2]))
                v.tensor_scalar(xn[:, :], x_sb[:, :], mv[:, 0:1], vstd[:, 0:1], ALU.subtract, ALU.mult
                                ).then_inc(xn_ready, 1)

            def take_xnT(n, i):
                dve_.wait_ge(xnT_ps, n + 1)
                v.tensor_copy(xnT[:, :, :].rearrange("p k l -> p (k l)"), bk(i, D)).then_inc(xnT_ready, 1)

            dve_.wait_ge(s_x, 16)
            layer_norm(0)
            take_xnT(0, 7)
            for n in range(2):
                dve_.wait_ge(q_ps, n + 1)
                v.tensor_copy(qT[:, 4 * n:4 * n + 4, :].rearrange("p j l -> p (j l)"), bk(4 + n)).then_inc(q_ready, 1)
            dve_.wait_ge(ids, 3)
            v.tensor_copy(iota_f[:, :], iota_i[:, :])
            v.tensor_copy(ones_r[:, :], ones[:, :])
            v.memset(mold[:, :], -3.0e38).then_inc(mold_ready, 1)
            for n in range(2 * NG):
                sl = slice(n % NG * BANK, (n % NG + 1) * BANK)
                dve_.wait_ge(Ahi_ready, n + 1)
                v.tensor_tensor(A_lo[:, n // NG, sl], bk(n), A_hi[:, n // NG, sl].bitcast(F32), ALU.subtract
                                ).then_inc(A_ready, 1)

            def split_lo(i, p):
                n = tiles_of(p)
                dve_.wait_ge(ctxhi_ready, i * PAIRS + (p + 1))
                hi, lo = [ctxT[:, 2 * p:2 * p + n, s, :, :].rearrange("p j k r -> p j (k r)") for s in range(2)]
                v.tensor_tensor(lo, bk(5, n * D).rearrange("p (j n) -> p j n", j=n), hi.bitcast(F32),
                                ALU.subtract).then_inc(ctxlo_ready, 1)

            dve_.wait_ge(s_wv, 16)
            link(v.tensor_copy(Wv_hi[:, :, :], Wv_sb))
            v.tensor_tensor(Wv_lo[:, :, :], Wv_sb, Wv_hi[:, :, :].bitcast(F32), ALU.subtract).then_inc(wv_ready, 1)
            v.tensor_reduce(amax[:, 0:1], Wv_sb.rearrange("p k n -> p (k n)"), AX_X, ALU.max,
                            apply_absolute_value=True).then_inc(wmax_ready, 1)

            def take_squares(i):
                dve_.wait_ge(sq_ps, i + 1)
                v.tensor_reduce(bound[:, 0:1], bk(5, SQ), AX_X, ALU.add).then_inc(sig_own, 1)

            take_squares(0)
            for p in range(PAIRS):
                split_lo(0, p)

            dve_.wait_ge(gmax_ready, 1)
            link(v.tensor_tensor(wmax[:, 1:2], wmax[:, 0:1], wmax[:, 0:1], ALU.mult))

            def bound_values(i):
                first = isinstance(i, int)
                dve_.wait_ge(sig_own, i * SIG_OWN + 1)
                if first:
                    v.tensor_copy(bound[:, 1:2], bound[:, 0:1]).then_inc(sig_own, 1)
                else:
                    v.tensor_tensor(bound[:, 1:2], bound[:, 1:2], bound[:, 0:1], ALU.add).then_inc(sig_own, 1)
                dve_.wait_ge(sig_own, i * SIG_OWN + 2)
                v.tensor_scalar(bound[:, 2:3], bound[:, 1:2], wmax[:, 1:2], 1e-30, ALU.mult, ALU.max).then_inc(sig_own, 1)
                dve_.wait_ge(sig_own, i * SIG_OWN + 3)
                v.reciprocal(bound[:, 3:4], bound[:, 2:3]).then_inc(sig_own, 1)
                dve_.wait_ge(sig_own, i * SIG_OWN + 4)
                v.tensor_scalar(bound[:, 2:3], bound[:, 3:4], 2048.0 ** 2, None, ALU.mult).then_inc(sig_own, 1)
                dve_.wait_ge(sig_own, i * SIG_OWN + 5)
                b = bound[:, :].bitcast(I32)
                v.tensor_scalar(b[:, 3:4], b[:, 2:3], 0x7F800000, 1, ALU.bitwise_and, ALU.logical_shift_right
                                ).then_inc(sig_own, 1)
                dve_.wait_ge(sig_own, i * SIG_OWN + 6)
                v.tensor_scalar(b[:, 2:3], b[:, 3:4], 127 << 22, None, ALU.add).then_inc(sig_own, 1)

            def scale_values(i):
                dve_.wait_ge(sig_own, i * SIG_OWN + SIG_OWN)
                v.tensor_scalar(sigma[:, :].bitcast(I32), bound[:, 2:3].bitcast(I32), 0x7F800000, None,
                                ALU.bitwise_and).then_inc(sig_ready, 1)

            bound_values(0)
            scale_values(0)
            dve_.wait_ge(sig_ready, 1)
            v.reciprocal(sigma_inv[:, :], sigma[:, :]).then_inc(inv_ready, 1)
            v.memset(rho[:, :], 1.0).then_inc(rho_ready, 1)

            def block_(i, first=False, ahead=True, last=False):
                for k in range(STEPS if not last else SUM - CT + 1):
                    pair = None if last else pair_at(i, k, 1, first, ahead)
                    if pair:
                        split_lo(*pair)
                    u = late_unit(i, k, MAX, first, last)
                    if u:
                        hs4 = slice(u[1] * GH, (u[1] + 1) * GH)
                        dve_.wait_ge(turned, u[0] + 1)
                        v.tensor_reduce(blkmax[:, hs4], bk(6).rearrange("p (h r) -> p h r", r=P), AX_X, ALU.max
                                        ).then_inc(blkmax_ready, 1)
                        dve_.wait_ge(blkmax_ready, u[0] + 1)
                        dve_.wait_ge(mold_ready, u[0] + 1)
                        v.tensor_tensor(mnew[:, hs4], mold[:, hs4], blkmax[:, hs4], ALU.max).then_inc(mnew_ready, 1)
                        dve_.wait_ge(mnew_ready, u[0] + 1)
                        if not (first and u[1] < 1):
                            dve_.wait_ge(mrow_ps, u[0])
                        v.tensor_tensor(diag[:, :, :], ident[:, :].unsqueeze(1).broadcast_to([P, GH, P]),
                                        mnew[:, hs4].bitcast(F32).unsqueeze(2).broadcast_to([P, GH, P]), ALU.mult
                                        ).then_inc(diag_ready, 1)
                    s = late(i, k, LESS, first, last)
                    if s:
                        if not (first and s[1] < 2):
                            dve_.wait_ge(exp_done, s[0] - 1)
                        if s[1] % CT == 0:
                            dve_.wait_ge(mrow_ready, i * NG + ((k - LESS) // CT + 1))
                        v.tensor_tensor(dbuf[s[1] % 2], ring[:, s[1] % RING, :], mrow[s[1] // CT % 2], ALU.subtract
                                        ).then_inc(d_ready, 1)
                    g, j = k // CT, k % CT
                    if not last:
                        dve_.wait_ge(copied, i * STEPS + (k + 1))
                        if j:
                            if j == 1:
                                if not (first and g < 2):
                                    dve_.wait_ge(turned, i * NG + (g - 1))
                            else:
                                dve_.wait_ge(topped, i * (NG * (CT - 1)) + (g * (CT - 1) + j - 1))
                            v.tensor_tensor(tops[g % 2], ring[:, (k - 1) % RING, :] if j == 1 else tops[g % 2],
                                            ring[:, k % RING, :], ALU.max).then_inc(topped, 1)
                        if k == 0 and not first:
                            dve_.wait_ge(sig_ready, i + 1)
                        if k == RHO_STEP and not first:
                            dve_.wait_ge(shrunk, i * NG)
                            dve_.wait_ge(inv_ready, i)
                            v.tensor_tensor(rho[:, :], sigma[:, :], sigma_inv[:, :], ALU.mult).then_inc(rho_ready, 1)
                            dve_.wait_ge(rho_ready, i + 1)
                            v.reciprocal(sigma_inv[:, :], sigma[:, :]).then_inc(inv_ready, 1)
                        if k == SQ_SUM + 1 and ahead:
                            take_squares(i + 1)
                            bound_values(i + 1)
                        if k == STEPS - 1 and ahead:
                            dve_.wait_ge(vlo_ready, i * RING + RING)
                            scale_values(i + 1)
                        if k % 2 == 0:
                            half, jj = k // RING, k % RING // 2
                            dve_.wait_ge(vhi_ready, i * RING + (k // 2 + 1))
                            v.scalar_tensor_tensor(V_lo[:, jj, half * 8:half * 8 + 8, 0:DH],
                                                   values_at(k // 2).rearrange("p (h d) -> p h d", d=DH), sigma[:, :],
                                                   V_hi[:, jj, half * 8:half * 8 + 8, 0:DH], ALU.mult, ALU.subtract
                                                   ).then_inc(vlo_ready, 1)
                    s = late(i, k, LOW, first, last)
                    if s:
                        dve_.wait_ge(exp_done, s[0] + 1)
                        v.tensor_tensor(P_lo[:, s[1] % PR, :], pfull[s[1] % 2], P_hi[:, s[1] % PR, :], ALU.subtract
                                        ).then_inc(p_ready, 1)
                    u = late_unit(i, k, SUM, first, last)
                    if u:
                        dve_.wait_ge(pv_done, u[0] * CT + CT)
                        dve_.wait_ge(shrunk, u[0] + 1)
                        of_unit = Oacc[:, u[1] * GH:(u[1] + 1) * GH, 0:DH + 1]
                        v.tensor_tensor(of_unit, of_unit,
                                        bk(3 + u[1] % 2, GH * (DH + 1)).rearrange("p (h d) -> p h d", h=GH),
                                        ALU.add).then_inc(summed, 1)

            block_(0, first=True)
            with dve_.Fori(1, NC - 1) as i:
                block_(i)
            block_(NC - 1, ahead=False)
            block_(NC, last=True)

            dve_.wait_ge(summed, NC * NG)
            link(v.tensor_scalar(den[:, 0:H], Oacc[:, :, DH], sigma[:, :], None, ALU.mult))
            link(v.reciprocal(den[:, H:2 * H], den[:, 0:H]))
            for n in range(2):
                hs8 = slice(n * 8, n * 8 + 8)
                v.tensor_tensor(O.rearrange("p (h d) -> p h d", d=DH)[:, hs8], Oacc[:, hs8, 0:DH],
                                den[:, H + n * 8:H + n * 8 + 8].unsqueeze(2).broadcast_to([P, 8, DH]), ALU.mult
                                ).then_inc(O_ready, 1)
            dve_.wait_ge(xa_ps, 1)
            link(v.tensor_tensor(x_sb[:, :], x_sb[:, :], bk(2, D), ALU.add))

            layer_norm(1)
            take_xnT(1, 3)
            dve_.wait_ge(qkv_ps, 2)
            dve_.wait_ge(vone_ready, 2)
            v.tensor_copy(va[:, :, 0:HD], bk(5, D).rearrange("p (h d) -> p h d", d=HD)).then_inc(qkv_ready, 1)

            def negative(n):
                skip_first(dve_, fexp_ready, n - 1)
                dve_.wait_ge(feat_ps, n + 1)
                v.tensor_scalar(fneg[n % 2], bk(n), 0.0, None, ALU.min).then_inc(neg_ready, 1)

            def feature(n):
                dst = (kp, qp)[n // 4][n % 4 // 2][:, n % 2 * BANK:(n % 2 + 1) * BANK]
                dve_.wait_ge(fexp_ready, n + 1)
                v.scalar_tensor_tensor(dst, bk(n), 0.0, fexp[n % 2], ALU.max, ALU.add).then_inc(feat_ready, 1)

            negative(0)
            for n in range(8):
                if n < 7:
                    negative(n + 1)
                feature(n)
            dve_.wait_ge(kv_ps, 1)
            v.tensor_copy(kv[:, :, 0:HD + 1], bk(0, H * (HD + 1)).rearrange("p (h d) -> p h d", d=HD + 1)
                          ).then_inc(kv_ready, 1)
            dve_.wait_ge(at_ps, 1)
            atp = bk(1, H * (HD + 1)).rearrange("p (h d) -> p h d", d=HD + 1)
            link(v.tensor_scalar(den[:, 0:H], atp[:, :, HD], 1e-8, None, ALU.add))
            link(v.reciprocal(den[:, H:2 * H], den[:, 0:H]))
            v.tensor_tensor(xn[:, :].rearrange("p (h d) -> p h d", d=HD), atp[:, :, 0:HD],
                            den[:, H:2 * H].unsqueeze(2).broadcast_to([P, H, HD]), ALU.mult).then_inc(at_ready, 1)
            dve_.wait_ge(atT_ps, 1)
            v.tensor_copy(xnT[:, :, :].rearrange("p k l -> p (k l)"), bk(2, D)).then_inc(atT_ready, 1)
            dve_.wait_ge(sa_ps, 1)
            link(v.tensor_tensor(x_sb[:, :], x_sb[:, :], bk(3, D), ALU.add))

            layer_norm(2)
            take_xnT(2, 4)
            dve_.wait_ge(lg_ps, 1)
            link(v.tensor_copy(lg[:, 0, :], bk(5, NE)))
            link(v.tensor_reduce(small[:, 0:1], lg[:, 0, :], AX_X, ALU.max))
            v.tensor_scalar(small[:, 1:2], small[:, 0:1], -1.0, None, ALU.mult).then_inc(lmax_ready, 1)
            link(v.tensor_scalar(lg[:, 2, :], lg[:, 0, :], small[:, 0:1], None, ALU.is_ge))
            link(v.scalar_tensor_tensor(lg[:, 3, :], lg[:, 2, :], -64.0, iota_f[:, 0:NE], ALU.mult, ALU.add))
            link(v.tensor_reduce(small[:, 4:5], lg[:, 3, :], AX_X, ALU.min))
            v.tensor_scalar(lg[:, 4, :], lg[:, 3, :], small[:, 4:5], None, ALU.is_equal).then_inc(mask_ready, 1)
            dve_.wait_ge(lexp_ready, 1)
            link(v.reciprocal(small[:, 3:4], small[:, 2:3]))
            link(v.tensor_scalar(lg[:, 1, :], lg[:, 1, :], small[:, 3:4], None, ALU.mult))
            dve_.wait_ge(rank_ps, 1)
            link(v.scalar_tensor_tensor(lg[:, 4, :], bk(6, NE), CAP + 0.5, lg[:, 4, :], ALU.is_lt, ALU.mult))
            link(v.scalar_tensor_tensor(lg[:, 5, :], bk(6, NE), -1.0, lg[:, 4, :], ALU.add, ALU.mult))
            link(v.tensor_reduce(small[:, 5:6], lg[:, 5, :], AX_X, ALU.add))
            link(v.tensor_tensor(lg[:, 6, :], lg[:, 4, :], lg[:, 1, :], ALU.mult))
            link(v.tensor_scalar(oh, iota_f[:, :], small[:, 5:6], None, ALU.is_equal))
            link(v.tensor_tensor(comb.rearrange("p (e c) -> p e c", c=CS),
                                 lg[:, 6, :].unsqueeze(2).broadcast_to([P, NE, CS]),
                                 oh.unsqueeze(1).broadcast_to([P, NE, CS]), ALU.mult))
            v.tensor_scalar(disp, comb, 0.0, None, ALU.is_gt).then_inc(comb_ready, 1)

            def gelu(q):
                dve_.wait_ge(hcopy_ready, 2 * q + 2)
                link(v.tensor_scalar(hg, hg, GELU_B, 1.0, ALU.mult, ALU.add))
                skip_first(dve_, hT_ps, q)
                v.tensor_tensor(hh, hg, hs, ALU.mult).then_inc(u_ready, 1)
                dve_.wait_ge(tanh_ready, q + 1)
                v.scalar_tensor_tensor(hh, hg, 1.0, hs, ALU.add, ALU.mult).then_inc(g_ready, 1)

            def take_y(q):
                skip_first(dve_, y_summed, q)
                dve_.wait_ge(unit_used, down_done[q])
                v.tensor_copy(y, bk(6, D)).then_inc(y_ready, 1)

            for q in range(NQ):
                gelu(q)
                take_y(q)
            dve_.wait_ge(y_summed, NQ)
            v.tensor_tensor(res, x_sb[:, :], bk(7, D), ALU.add).then_inc(res_ready, 1)

        @block.tensor
        def _(pe):
            def mm(out_, lhsT, rhs, start=True, stop=True):
                return pe.matmul(out_, lhsT, rhs, start=start, stop=stop, skip_group_check=True)

            pe.wait_ge(ids, 1)
            pe.wait_ge(s_wk, 16)
            for g in range(4):
                for j in range(2 * g, 2 * g + 2):
                    for k in range(KH):
                        ins = pe.transpose(bk(g)[:, (j % 2 * KH + k) * P:(j % 2 * KH + k + 1) * P],
                                           Wk_sb[:, k, j * P:(j + 1) * P], ident[:, :])
                ins.then_inc(wkT_ps, 1)

            def transpose_tokens(n, i):
                pe.wait_ge(xn_ready, n + 1)
                for k in range(KH):
                    ins = pe.transpose(bk(i)[:, k * P:(k + 1) * P], xn[:, k * P:(k + 1) * P], ident[:, :])
                ins.then_inc(xnT_ps, 1)
                pe.wait_ge(xnT_ready, n + 1)

            transpose_tokens(0, 7)
            pe.wait_ge(s_wq, 16)
            for j in range(HP):
                for k in range(KH):
                    ins = mm(bk(4 + j // 4)[:, j % 4 * P:(j % 4 + 1) * P], Wq_sb[:, k, j * P:(j + 1) * P],
                             xnT[:, k, :], k == 0, k == KH - 1)
                if j % 4 == 3:
                    ins.then_inc(q_ps, 1)
            pe.wait_ge(wkT_ready, 4)
            pe.wait_ge(q_ready, 2)
            for r in (0, DH):
                if r:
                    pe.wait_ge(A_even, 1)
                for k in range(KH):
                    for g in range(NG):
                        for h in range(g * GH + r // DH, (g + 1) * GH, 2):
                            ins = mm(bk(k * NG + g)[:, h % GH * P:(h % GH + 1) * P],
                                     WkT[r:r + DH, h // 2, k * P:(k + 1) * P], qT[r:r + DH, h // 2, :])
                        if r:
                            ins.then_inc(A_ps, 1)
                if not r:
                    ins.then_inc(A_even, 1)
            pe.wait_ge(A_ready, 2 * NG)

            def turn(i, p):
                pe.wait_ge(raw_loaded, i * 16 + 16)
                if p:
                    pe.wait_ge(ctxlo_ready, i * PAIRS + p)
                else:
                    pe.wait_ge(sig_own, i * SIG_OWN + 1)
                for j in range(tiles_of(p)):
                    for k in range(KH):
                        ins = pe.transpose(bk(5)[:, (j * KH + k) * P:(j * KH + k + 1) * P],
                                           raw[:, 2 * p + j, k * P:(k + 1) * P], ident[:, :])
                ins.then_inc(tr_ready, 1)

            def sum_squares(i):
                if not isinstance(i, int):
                    pe.wait_ge(ctxlo_ready, i * PAIRS)
                pe.wait_ge(sq_done, i * SQ + SQ)
                mm(bk(5, SQ), ones[:, :], chsq[:, :]).then_inc(sq_ps, 1)

            pe.wait_ge(s_tail, 16 * (11 + H))
            for k in range(KH):
                for r in range(6):
                    n = k * 6 + r
                    pe.transpose(bk(4 + n // 4)[:, n % 4 * P:(n % 4 + 1) * P], Wqkv_sb[r][:, k * P:(k + 1) * P], ident[:, :])
            for k in range(KH):
                for r in range(2):
                    ins = pe.transpose(bk(7)[:, (k * 2 + r) * P:(k * 2 + r + 1) * P],
                                       Wout_sb[r][:, k * P:(k + 1) * P], ident[:, :])
            ins.then_inc(wT_ps, 1)
            pe.wait_ge(wT_ready, 1)
            for k in range(KH):
                ins = pe.transpose(bk(4)[:, k * NE:(k + 1) * NE], gate_sb[:, k * P:(k + 1) * P], ident[0:NE, 0:NE])
            ins.then_inc(wT_ps, 1)
            pe.wait_ge(wT_ready, 5)
            sum_squares(0)
            for p in range(PAIRS):
                turn(0, p)
            pe.wait_ge(wv_ready, 1)

            PARTS = ((0, 0), (0, 1), (1, 0))

            def values(i, n):
                if not (isinstance(i, int) and i == 0 and n < 2):
                    pe.wait_ge(vlo_ready, i * RING + (n - 1))
                half, j = n // CT, n % CT
                for m, (s, w) in enumerate(PARTS):
                    for k in range(KH):
                        ins = mm(values_at(n), ctxT[:, j, s, k, :], (Wv_hi, Wv_lo)[w][:, k, half * BANK:(half + 1) * BANK],
                                 m + k == 0, m + k == 3)
                ins.then_inc(v_ready, 1)

            def scores(i, k, first):
                g, j = k // CT, k % CT
                if g == 0:
                    pe.wait_ge(ctxlo_ready, i * PAIRS + (j // 2 + 1))
                if not (first and k < 2):
                    pe.wait_ge(copied, i * STEPS + (k - 1))
                for m, (s, w) in enumerate(PARTS):
                    for h in range(KH):
                        ins = mm(bk(k % 2), ctxT[:, j, s, h, :], (A_hi, A_lo)[w][:, h, g * BANK:(g + 1) * BANK],
                                 m + h == 0, m + h == 3)
                ins.then_inc(s_ready, 1)

            def weigh(i, b, first):
                g, j = b % STEPS // CT, b % CT
                pe.wait_ge(p_ready, i * STEPS + (b + 1))
                if g % 2 == 0:
                    pe.wait_ge(vlo_ready, i * RING + (b // STEPS * RING + g // 2 * CT + j + 1))
                if j == 0 and not (first and g < 2):
                    pe.wait_ge(summed, i * NG + (b // STEPS * NG + g - 1))
                r = b % PR
                for n in range(GH):
                    h = g * GH + n
                    hi, lo = P_hi[:, r, n * P:(n + 1) * P], P_lo[:, r, n * P:(n + 1) * P]
                    mm(acc_of(h), hi, V_hi[:, j, h, 0:DH + 1], j == 0 and n == 0, False)
                    mm(acc_of(h)[:, 0:DH], hi, V_lo[:, j, h, 0:DH], False, False)
                    ins = mm(acc_of(h), lo, V_hi[:, j, h, 0:DH + 1], False, False)
                ins.then_inc(pv_done, 1)

            def block_(i, first=False, ahead=True, last=False):
                for k in range(STEPS if not last else WEIGH + 2):
                    if not last:
                        if k == SQ_SUM and ahead:
                            sum_squares(i + 1)
                        pair = pair_at(i, k, 0, first, ahead)
                        if pair:
                            turn(*pair)
                        scores(i, k, first)
                    u = late_unit(i, k, DIAG, first, last)
                    if u:
                        pe.wait_ge(blkmax_ready, u[0] + 1)
                        pe.wait_ge(diag_ready, u[0] + 1)
                        mm(bk(6), ones_r[:, :], diag[:, :, :].rearrange("p h l -> p (h l)")).then_inc(mrow_ps, 1)
                    if not last:
                        if k % 2 == 0:
                            values(i, k // 2)
                    if k % 2:
                        for b in (k - WEIGH - 1, k - WEIGH):
                            if not (first and b < 0) and not (last and b >= 0):
                                weigh(i, b, first)
                    u = late_unit(i, k, TURN, first, last)
                    if u:
                        pe.wait_ge(topped, u[0] * (CT - 1) + (CT - 1))
                        if not (first and u[1] < 1):
                            pe.wait_ge(mrow_ready, u[0])
                        for n in range(GH):
                            ins = pe.transpose(bk(6)[:, n * P:(n + 1) * P], tops[u[1] % 2][:, n * P:(n + 1) * P], ident[:, :])
                        ins.then_inc(turned, 1)

            block_(0, first=True)
            with pe.Fori(1, NC - 1) as i:
                block_(i)
            block_(NC - 1, ahead=False)
            block_(NC, last=True)

            for j in range(HP):
                if j % 4 == 0:
                    pe.wait_ge(O_ready, j // 4 + 1)
                ins = pe.transpose(bk(j // 4)[:, j % 4 * P:(j % 4 + 1) * P], O[:, j * P:(j + 1) * P], ident[:, :])
                if j % 4 == 3:
                    ins.then_inc(OT_ps, 1)
            for j in range(HP):
                if j % 4 == 0:
                    pe.wait_ge(OT_ready, j // 4 + 1)
                ins = mm(bk(2, D), OT[:, j, :], Wo_sb[:, j, :], j == 0, j == HP - 1)
            ins.then_inc(xa_ps, 1)

            transpose_tokens(1, 3)
            for j in range(4):
                for k in range(KH):
                    ins = mm(bk(4)[:, j * P:(j + 1) * P], WqkvT[:, k, j * P:(j + 1) * P], xnT[:, k, :], k == 0, k == KH - 1)
            ins.then_inc(qkv_ps, 1)
            for k in range(KH):
                ins = mm(bk(5, D), xnT[:, k, :], WqkvT[:, k, 2 * D:3 * D], k == 0, k == KH - 1)
            ins.then_inc(qkv_ps, 1)
            pe.wait_ge(qkv_ready, 2)
            for n in range(4):
                mm(bk(n), qkT[:, 2 + n // 2, :], bd[:, n // 2, n % 2 * BANK:(n % 2 + 1) * BANK]).then_inc(feat_ps, 1)
            for n in range(4):
                for h in range(4 * n, 4 * n + 4):
                    ins = mm(bk(4 + n)[:, h % 4 * P:(h % 4 + 1) * P], bd[:, h // 8, h % 8 * F:(h % 8 + 1) * F],
                             qkT[:, h // 8, :])
                ins.then_inc(feat_ps, 1)
            pe.wait_ge(feat_ready, 4)
            for h in range(H):
                ins = mm(bk(0)[:, h * (HD + 1):(h + 1) * (HD + 1)], kp[h // 8][:, h % 8 * F:(h % 8 + 1) * F],
                         va[:, h, 0:HD + 1])
            ins.then_inc(kv_ps, 1)
            pe.wait_ge(feat_ready, 8)
            pe.wait_ge(kv_ready, 1)
            for h in range(H):
                ins = mm(bk(1)[:, h * (HD + 1):(h + 1) * (HD + 1)], qp[h // 8][:, h % 8 * P:(h % 8 + 1) * P],
                         kv[:, h, 0:HD + 1])
            ins.then_inc(at_ps, 1)
            pe.wait_ge(at_ready, 1)
            for k in range(KH):
                ins = pe.transpose(bk(2)[:, k * P:(k + 1) * P], xn[:, k * P:(k + 1) * P], ident[:, :])
            ins.then_inc(atT_ps, 1)
            pe.wait_ge(atT_ready, 1)
            for k in range(KH):
                mm(bk(3, D), xnT[:, k, :], WoutT[:, k, :], k == 0, False)
            mm(bk(3, D), ones[0:1, :], b_sb[:, :], False, True).then_inc(sa_ps, 1)

            transpose_tokens(2, 4)
            for k in range(KH):
                ins = mm(bk(5, NE), xnT[:, k, :], gateT[:, k, :], k == 0, k == KH - 1)
            ins.then_inc(lg_ps, 1)
            pe.wait_ge(mask_ready, 1)
            mm(bk(6, NE), upper[:, :], lg[:, 4, :]).then_inc(rank_ps, 1)
            pe.wait_ge(comb_ready, 1)
            for k in range(KH):
                mm(bk(k), xn[:, k * P:(k + 1) * P], disp).then_inc(disp_ps, 1)
            for q in range(NQ):
                ins = pe.transpose(bk(2)[:, q * P:(q + 1) * P], comb[:, q * P:(q + 1) * P], ident[:, :])
            ins.then_inc(disp_ps, 1)
            pe.wait_ge(disp_ready, 2)
            pe.wait_ge(combT_ready, 1)

            done = [0]

            def next_unit():
                n = done[0]
                done[0] += 1
                pe.wait_ge(unit_loaded[n % UNITS], 16 * (n // UNITS + 1))
                return unit[n % UNITS]

            def up(q):
                skip_first(pe, hcopy_ready, 2 * (q - 1))
                for j in range(QE):
                    w = next_unit().rearrange("p (k f) -> p k f", k=KH)
                    c0 = (q * QE + j) * CS
                    for half in range(2):
                        for k in range(KH):
                            ins = mm(bank[q % 2][j * CS:(j + 1) * CS, half, :], dispT[:, k, c0:c0 + CS],
                                     w[:, k, half * BANK:(half + 1) * BANK], k == 0, k == KH - 1)
                    ins.then_inc(unit_used, 1)

            def turn_hidden(q):
                pe.wait_ge(g_ready, q + 1)
                skip_first(pe, hT_ready, q)
                for t in range(FT):
                    ins = pe.transpose(bank[2][:, t // 4, t % 4 * P:(t % 4 + 1) * P], hh[:, t * P:(t + 1) * P], ident[:, :])
                ins.then_inc(hT_ps, 1)

            def down(q):
                pe.wait_ge(hT_ready, q + 1)
                skip_first(pe, y_ready, q)
                for j in range(QE):
                    w = next_unit().rearrange("p (t d) -> p t d", t=FT)
                    for t in range(FT):
                        ins = mm(bk(6)[j * CS:(j + 1) * CS, 0:D], hT[:, t, j * CS:(j + 1) * CS], w[:, t, :],
                                 t == 0, t == FT - 1)
                    ins.then_inc(unit_used, 1)

            def combine(q):
                pe.wait_ge(y_ready, q + 1)
                mm(bk(7, D), combT[:, q, :], y, q == 0, q == NQ - 1).then_inc(y_summed, 1)

            up(0)
            for q in range(NQ):
                if q + 1 < NQ:
                    up(q + 1)
                turn_hidden(q)
                if q > 0:
                    combine(q - 1)
                down(q)
            combine(NQ - 1)


_INS = ["x", "ctx_1024", "L0_xattn_Wq", "L0_xattn_Wk", "L0_xattn_Wv", "L0_xattn_Wo", "L0_attn_W_qkv",
        "L0_attn_proj", "L0_attn_W_out", "L0_attn_b_out", "L0_ffn_gate_w", "L0_ffn_w1", "L0_ffn_w2"]
_OUTS = [((1, 128, 256), "float32")]


def kernel(**inputs):
    import numpy as _np
    import concourse.bacc as _bacc
    from concourse import mybir as _mybir
    from concourse.bass_utils import run_bass_kernel_spmd as _run

    nc = _bacc.Bacc("TRN2", target_bir_lowering=False, num_devices=1)
    arrays, args = {}, []
    for name in _INS:
        a = _np.ascontiguousarray(inputs[name])
        arrays[f"in_{name}_dram"] = a
        args.append(nc.dram_tensor(f"in_{name}_dram", a.shape, _mybir.dt.from_np(a.dtype), kind="ExternalInput").ap())
    for i, (shape, dtype) in enumerate(_OUTS):
        dt = _mybir.dt.from_np(_np.dtype(dtype))
        args.append(nc.dram_tensor(f"out_{i}_dram", shape, dt, kind="ExternalOutput").ap())
    perceiver_layer(nc, *args)
    r = _run(nc, [arrays], core_ids=[0])
    got = tuple(r.results[0][f"out_{i}_dram"] for i in range(len(_OUTS)))
    return got[0]
```

```python
from contextlib import ExitStack

import concourse.bass as bass
from concourse import mybir

ALU = mybir.AluOpType
ACT = mybir.ActivationFunctionType
AX_X = mybir.AxisListType.X
F32 = mybir.dt.float32
F32R = mybir.dt.float32r
F16 = mybir.dt.float16
I32 = mybir.dt.int32
RMAX = bass.bass_isa.ReduceOp.max

P = 128
D = 256
KH = D // P
H = 16
DH = 64
INNER = H * DH
HP = H // 2
HD = D // H
F = 128
BANK = 512
GH = BANK // P
NG = H // GH
CT = 7
PAIRS = (CT + 1) // 2
STEPS = CT * NG
RING = 2 * CT
LESS = 12
EXP = 13
LOW = 14
WEIGH = 16
BURST = 4
TURN = 8
MAX = 9
DIAG = 11
ROW = 11
SUM = 26
SQ = 4
SQ_STEP = 9
SQ_SUM = 18
RHO_STEP = 10
SIG_OWN = 7
PR = 7
VW = DH + 2
VS = HD + 2
NE = 16
FF = 1024
FT = FF // P
CAP = 10
CS = 32
QE = P // CS
NQ = NE // QE
LOG_PSCALE = 11 * 0.6931471805599453
SCALE = DH ** -0.5
EPS = 1e-5
GELU_A = 0.7978845608028654
GELU_B = 0.044715
LATE_UNITS = 8


def perceiver_layer(nc, x, ctx_in, Wq, Wk, Wv, Wo, W_qkv, proj, W_out, b_out, gate_w, w1, w2, out):
    R = ctx_in.shape[1]
    NT = R // P
    NC = NT // CT
    assert R % (P * CT) == 0 and NC >= 3 and x.shape[1] == P
    assert CAP == max(int(1.25 * P / NE) + int(1.25 * P / NE) % 2, 4)

    with ExitStack() as ctx:
        def sb(name, shape, dt=F32):
            return ctx.enter_context(nc.sbuf_tensor(name, shape, dt))

        def sem(name):
            return ctx.enter_context(nc.semaphore(name))

        bank = [ctx.enter_context(nc.psum_tensor(f"pair{i}", [P, 2, BANK], F32)) for i in range(4)]

        def bk(i, n=BANK):
            return bank[i // 2][:, i % 2, 0:n]

        with ExitStack() as over:
            def operand(name, shape):
                return over.enter_context(nc.sbuf_tensor(name, shape, F32R))

            A_hi = operand("A_hi", [P, KH, H * P])
            A_lo = operand("A_lo", [P, KH, H * P])
            Wv_hi = operand("Wv_hi", [P, KH, INNER])
            Wv_lo = operand("Wv_lo", [P, KH, INNER])
            ctxT = operand("ctxT", [P, CT, 2, KH, P])
        EARLY_UNITS = (2 * KH * H * P + 2 * KH * INNER + CT * 2 * D) // (KH * FF)
        early = sb("early", [P, 2 * KH * H * P + 2 * KH * INNER + CT * 2 * D])
        ident = sb("ident", [P, P])
        upper = sb("upper", [P, P])
        ones = sb("ones", [P, P])
        ones_r = sb("ones_r", [P, P], F32R)
        iota_f = sb("iota_f", [P, CS])
        diag = sb("diag", [P, GH, P], F32R)
        mnew = sb("mnew", [P, H], F32R)
        Vall = sb("Vall", [P, CT * 2 * H * VW], F16)
        V_hi, V_lo = [Vall[:, :].rearrange("p (s j h d) -> p s j h d", s=2, j=CT, h=H)[:, n] for n in range(2)]
        Pall = sb("Pall", [P, 2 * PR * BANK], F16)
        P_hi, P_lo = [Pall[:, :].rearrange("p (s r n) -> p s r n", s=2, r=PR)[:, n] for n in range(2)]
        Oacc = sb("Oacc", [P, H, VW])
        late_mem = sb("late_mem", [P, LATE_UNITS * KH * FF])
        unit = [early[:, n * KH * FF:(n + 1) * KH * FF] for n in range(EARLY_UNITS)]
        unit += [late_mem[:, n * KH * FF:(n + 1) * KH * FF] for n in range(LATE_UNITS)]
        place = [0]

        def part(n, at=None):
            at = place[0] if at is None else at
            place[0] = at + n
            return late_mem[:, at:at + n]

        ring = part(RING * BANK).rearrange("p (r n) -> p r n", n=BANK)
        dbuf = [part(BANK) for n in range(2)]
        pfull = [part(BANK) for n in range(2)]
        tops = [part(BANK) for n in range(2)]
        mrow = [part(BANK) for n in range(2)]
        raw = part(CT * D).rearrange("p (j k) -> p j k", j=CT)
        qT = part(HP * P).rearrange("p (j l) -> p j l", l=P)
        Wqkv_sb = [part(D) for r in range(6)]
        Wout_sb = [part(D) for r in range(2)]
        gate_sb = part(D)[0:NE]
        assert place[0] <= LATE_UNITS * KH * FF
        Wq_sb = part(KH * INNER, 0).rearrange("p (k n) -> p k n", k=KH)
        Wk_sb = part(KH * INNER).rearrange("p (k n) -> p k n", k=KH)
        WkT = part(KH * INNER).rearrange("p (j k) -> p j k", j=HP)
        Wv_sb = part(KH * INNER).rearrange("p (k n) -> p k n", k=KH)
        iota_i = part(CS).bitcast(I32)
        Vf = Vall[:, :].bitcast(F32)
        Pf = Pall[:, :].bitcast(F32)
        Wo_sb = sb("Wo_sb", [P, HP, D])
        WT = sb("WT", [P, KH * 4 * D])
        WqkvT = WT[:, 0:KH * 3 * D].rearrange("p (k n) -> p k n", k=KH)
        WoutT = WT[:, KH * 3 * D:KH * 4 * D].rearrange("p (k n) -> p k n", k=KH)
        gateT = sb("gateT", [P, KH, NE])
        bd = sb("bd", [P, KH, 8 * F])
        b_sb = sb("b_sb", [1, D])
        unit += [Wo_sb[:, :, :].rearrange("p j d -> p (j d)"), bd[:, :, :].rearrange("p k n -> p (k n)"),
                 Pf[:, 0:KH * FF], WT[:, :]]
        UNITS = len(unit)
        assert HP * D == KH * FF and KH * 8 * F == KH * FF
        x_sb = sb("x_sb", [P, D])
        xn = sb("xn", [P, D])
        xnT = sb("xnT", [P, KH, P])
        columns = sb("columns", [P, 32])
        used = [0]

        def column(n):
            used[0] += n
            return columns[:, used[0] - n:used[0]]

        st = column(6)
        mv = column(2)
        vstd = column(2)
        mold = sb("mold", [P, H])
        blkmax = sb("blkmax", [P, H])
        fall = sb("fall", [P, H])
        alpha = sb("alpha", [P, H])
        with ExitStack() as over:
            xn_split = over.enter_context(nc.sbuf_tensor("xn_split", [P, 2, D], F32R))
        squares = sb("squares", [P, 2 * D])[:, 0:CT * D // SQ]
        chsq = column(SQ)
        amax = column(1)
        wmax = column(2)
        bound = column(4)
        sigma = column(1)
        sigma_inv = column(1)
        rho = column(1)
        lnp = column(1)
        den = Pf[:, 5 * BANK + 8 * NE:5 * BANK + 8 * NE + 2 * H]
        O = Vf[:, 0:INNER]
        OT = Vf[:, INNER:2 * INNER].rearrange("p (j l) -> p j l", j=HP)
        free = 2 * INNER
        qkT = Vf[:, free + 4096:free + 4096 + 4 * P].rearrange("p (j l) -> p j l", j=4)
        va = Vf[:, free + 4608 + H * VS:free + 4608 + 2 * H * VS].rearrange("p (h d) -> p h d", h=H)
        kv = Vf[:, free + 4608:free + 4608 + H * VS].rearrange("p (h d) -> p h d", h=H)
        qp = Vf[:, free:free + 1024], Vf[:, free + 1024:free + 2048]
        kp = Vf[:, free + 2048:free + 3072], Vf[:, free + 3072:free + 4096]
        fneg = Pf[:, 0:BANK], Pf[:, BANK:2 * BANK]
        fexp = Pf[:, 2 * BANK:3 * BANK], Pf[:, 3 * BANK:4 * BANK]
        lg = Pf[:, 5 * BANK:5 * BANK + 8 * NE].rearrange("p (r e) -> p r e", r=8)
        small = Pf[:, 6 * BANK + CS:6 * BANK + CS + 8]
        oh = Pf[:, 6 * BANK:6 * BANK + CS]
        of = Oacc[:, :, :].rearrange("p h d -> p (h d)")
        comb = of[:, 0:NE * CS]
        disp = diag[:, :, :].rearrange("p h l -> p (h l)")
        assert GH * P == NE * CS
        dispT = O.rearrange("p (k n) -> p k n", k=KH)
        combT = Vf[:, INNER:INNER + NE * CS].rearrange("p (q s) -> p q s", q=NQ)
        hh = qp
        hg = kp[0], Vf[:, free + 4096:free + 5120]
        hT = kp[1].rearrange("p (t n) -> p t n", t=FT)
        y = Pf[:, 4 * BANK:4 * BANK + D]
        res = Pf[:, 4 * BANK + D:4 * BANK + 2 * D]

        ids = sem("ids")
        s_x = sem("s_x")
        s_wq = sem("s_wq")
        s_wk = sem("s_wk")
        s_wv = sem("s_wv")
        s_tail = sem("s_tail")
        s_rest = sem("s_rest")
        bd_zero = sem("bd_zero")
        dve = sem("dve")
        phi_ready = sem("phi_ready")
        pool_own = sem("pool_own")
        var_ready = sem("var_ready")
        std_ready = sem("std_ready")
        xn_ready = sem("xn_ready")
        xnhi_ready = sem("xnhi_ready")
        xnlo_ready = sem("xnlo_ready")
        xnT_ps = sem("xnT_ps")
        xnT_ready = sem("xnT_ready")
        wkT_ps = sem("wkT_ps")
        wkT_ready = sem("wkT_ready")
        q_ps = sem("q_ps")
        q_ready = sem("q_ready")
        A_even = sem("A_even")
        A_ps = sem("A_ps")
        Ahi_ready = sem("Ahi_ready")
        A_ready = sem("A_ready")
        wvhi_ready = sem("wvhi_ready")
        wv_ready = sem("wv_ready")
        raw_loaded = sem("raw_loaded")
        sq_done = sem("sq_done")
        sq_ps = sem("sq_ps")
        sig_own = sem("sig_own")
        rho_ready = sem("rho_ready")
        inv_ready = sem("inv_ready")
        tr_ready = sem("tr_ready")
        ctxhi_ready = sem("ctxhi_ready")
        ctxlo_ready = sem("ctxlo_ready")
        copied = sem("copied")
        topped = sem("topped")
        turned = sem("turned")
        blkmax_ready = sem("blkmax_ready")
        mnew_ready = sem("mnew_ready")
        fall_ready = sem("fall_ready")
        diag_ready = sem("diag_ready")
        mold_ready = sem("mold_ready")
        alpha_ready = sem("alpha_ready")
        mrow_ps = sem("mrow_ps")
        mrow_ready = sem("mrow_ready")
        summed = sem("summed")
        shrunk = sem("shrunk")
        wT_ps = sem("wT_ps")
        wT_ready = sem("wT_ready")
        wmax_ready = sem("wmax_ready")
        gmax_ready = sem("gmax_ready")
        sig_ready = sem("sig_ready")
        vone_ready = sem("vone_ready")
        v_ready = sem("v_ready")
        vhi_ready = sem("vhi_ready")
        vlo_ready = sem("vlo_ready")
        s_ready = sem("s_ready")
        d_ready = sem("d_ready")
        exp_done = sem("exp_done")
        p_ready = sem("p_ready")
        pv_done = sem("pv_done")
        O_ready = sem("O_ready")
        OT_ps = sem("OT_ps")
        OT_ready = sem("OT_ready")
        xa_ps = sem("xa_ps")
        qkv_ps = sem("qkv_ps")
        qkv_ready = sem("qkv_ready")
        feat_ps = sem("feat_ps")
        neg_ready = sem("neg_ready")
        act_neg = sem("act_neg")
        fexp_ready = sem("fexp_ready")
        feat_ready = sem("feat_ready")
        kv_ps = sem("kv_ps")
        kv_ready = sem("kv_ready")
        at_ps = sem("at_ps")
        at_ready = sem("at_ready")
        atT_ps = sem("atT_ps")
        atT_ready = sem("atT_ready")
        sa_ps = sem("sa_ps")
        lg_ps = sem("lg_ps")
        lmax_ready = sem("lmax_ready")
        lexp_ready = sem("lexp_ready")
        mask_ready = sem("mask_ready")
        rank_ps = sem("rank_ps")
        comb_ready = sem("comb_ready")
        disp_ps = sem("disp_ps")
        disp_ready = sem("disp_ready")
        unit_loaded = [sem(f"unit_loaded{i}") for i in range(UNITS)]
        unit_used = sem("unit_used")
        y_summed = sem("y_summed")
        combT_ps = sem("combT_ps")
        combT_ready = sem("combT_ready")
        h2_ready = sem("h2_ready")
        u_ready = sem("u_ready")
        tanh_ready = sem("tanh_ready")
        g_ready = sem("g_ready")
        hT_ps = sem("hT_ps")
        hT_ready = sem("hT_ready")
        y_ready = sem("y_ready")
        res_ready = sem("res_ready")
        stored = sem("stored")

        x2d = x.rearrange("a n d -> (a n) d")
        out2d = out.rearrange("a n d -> (a n) d")
        ctx_chunks = ctx_in.rearrange("a (c j p) k -> (a c) p j k", j=CT, p=P)
        order = [(w1, 0)] + [(w, q) for q in range(1, NQ) for w, q in ((w1, q), (w2, q - 1))] + [(w2, NQ - 1)]
        units = [(w, q * QE + j) for w, q in order for j in range(QE)]
        up_done = [QE * ([(w is w1, n) for w, n in order].index((True, q)) + 1) for q in range(NQ)]
        down_done = [QE * ([(w is w1, n) for w, n in order].index((False, q)) + 1) for q in range(NQ)]
        T_LAST = NG * NT

        def skip_first(eng, semaphore, count):
            if not isinstance(count, int) or count > 0:
                eng.wait_ge(semaphore, count)

        def acc_of(h):
            return bk(3 + h // GH % 2)[:, h % GH * (DH + 1):(h % GH + 1) * (DH + 1)]

        FIRST_BANKS = (7, 0, 1, 2)

        def tiles_of(p):
            return min(2, CT - 2 * p)

        def pair_at(i, k, lag, first, ahead):
            for p in range(PAIRS):
                t = STEPS - CT + 1 + 3 * p + lag
                if k == t and ahead:
                    return i + 1, p
                if k == t - STEPS and not first:
                    return i, p
            return None

        def values_at(n):
            return bk((2, 7)[n % 2])

        def late(i, k, lag, first, last):
            b = k - lag
            if (first and b < 0) or (last and b >= 0):
                return None
            return i * STEPS + b, b % STEPS

        def late_unit(i, k, lag, first, last):
            b = k - lag
            if b % CT or (first and b < 0) or (last and b >= 0):
                return None
            return i * NG + b // CT, b // CT % NG

        block = ctx.enter_context(nc.Block())

        @block.sync
        def _(sp):
            sp.dma_start(x_sb[:, :], x2d).then_inc(s_x, 16)
            sp.dma_start(Wk_sb, Wk.rearrange("(k p) n -> p k n", p=P)).then_inc(s_wk, 16)
            sp.dma_start(Wq_sb, Wq.rearrange("(k p) n -> p k n", p=P)).then_inc(s_wq, 16)
            sp.dma_start(raw, ctx_chunks[0]).then_inc(raw_loaded, 16)
            sp.dma_start(Wv_sb, Wv.rearrange("(k p) n -> p k n", p=P)).then_inc(s_wv, 16)
            for r in range(6):
                sp.dma_start(Wqkv_sb[r], W_qkv[r * P:(r + 1) * P, :]).then_inc(s_tail, 16)
            for r in range(2):
                sp.dma_start(Wout_sb[r], W_out[r * P:(r + 1) * P, :]).then_inc(s_tail, 16)
            sp.dma_start(gate_sb, gate_w).then_inc(s_tail, 16)
            sp.dma_start(Wo_sb[:, :, :], Wo.rearrange("(j p) d -> p j d", p=P)).then_inc(s_rest, 16)
            sp.dma_start(b_sb[:, :], b_out.rearrange("(a d) -> a d", a=1)).then_inc(s_rest, 16)
            sp.wait_ge(bd_zero, 1)
            for h in range(H):
                r = h % 8 * HD
                sp.dma_start(bd[r:r + HD, h // 8, h % 8 * F:(h % 8 + 1) * F], proj[h]).then_inc(s_rest, 16)
            with sp.Fori(0, NC - 1) as i:
                sp.wait_ge(tr_ready, i * PAIRS + PAIRS)
                sp.wait_ge(sq_done, i * SQ + SQ)
                sp.dma_start(raw, ctx_chunks[i + 1]).then_inc(raw_loaded, 16)

            def load_unit(n):
                w, e = units[n]
                dst = unit[n % UNITS]
                if w is w1:
                    dst, src = dst.rearrange("p (k f) -> p k f", k=KH), w[e].rearrange("(k p) f -> p k f", p=P)
                else:
                    dst, src = dst.rearrange("p (t d) -> p t d", t=FT), w[e].rearrange("(t p) d -> p t d", p=P)
                sp.dma_start(dst, src).then_inc(unit_loaded[n % UNITS], 16)

            sp.wait_ge(s_ready, T_LAST)
            sp.wait_ge(v_ready, NC * RING)
            for n in range(EARLY_UNITS):
                load_unit(n)
            sp.wait_ge(p_ready, T_LAST)
            for n in range(EARLY_UNITS, UNITS - 4):
                load_unit(n)
            sp.wait_ge(xa_ps, 1)
            load_unit(UNITS - 4)
            sp.wait_ge(feat_ps, 8)
            load_unit(UNITS - 3)
            sp.wait_ge(feat_ready, 8)
            load_unit(UNITS - 2)
            sp.wait_ge(sa_ps, 1)
            load_unit(UNITS - 1)
            for n in range(UNITS, len(units)):
                sp.wait_ge(unit_used, n - UNITS + 1)
                load_unit(n)
            sp.wait_ge(res_ready, 1)
            sp.dma_start(out2d, res).then_inc(stored, 16)
            sp.wait_ge(stored, 16)

        @block.gpsimd
        def _(pool):
            pool.memset(ident[:, :], 0.0).then_inc(pool_own, 1)
            pool.memset(ones[:, :], 1.0).then_inc(pool_own, 1)
            pool.memset(bd[:, :, :], 0.0).then_inc(bd_zero, 1)
            pool.wait_ge(pool_own, 2)
            pool.affine_select(out=ident[:, :], in_=ident[:, :], compare_op=ALU.not_equal, fill=1.0,
                               base=0, pattern=[[-1, P]], channel_multiplier=1).then_inc(ids, 1)
            pool.affine_select(out=upper[:, :], in_=ones[:, :], compare_op=ALU.is_ge, fill=0.0,
                               base=0, pattern=[[1, P]], channel_multiplier=-1).then_inc(ids, 1)
            pool.iota(iota_i, pattern=[[1, CS]], base=0, channel_multiplier=0).then_inc(ids, 1)
            pool.memset(Oacc[:, :, :], 0.0).then_inc(ids, 1)
            pool.memset(lnp, LOG_PSCALE).then_inc(ids, 1)
            pool.memset(V_hi[:, :, :, DH:DH + 1], 1.0).then_inc(vone_ready, 1)
            pool.wait_ge(wmax_ready, 1)
            pool.partition_all_reduce(wmax[:, 0:1], amax[:, 0:1], P, RMAX).then_inc(gmax_ready, 1)

            def block_(i, first=False):
                for g in range(NG):
                    u = i * NG + g
                    hs4 = slice(g * GH, (g + 1) * GH)
                    pool.wait_ge(mnew_ready, u + 1)
                    pool.tensor_tensor(fall[:, hs4], mold[:, hs4], mnew[:, hs4].bitcast(F32), ALU.subtract
                                       ).then_inc(fall_ready, 1)
                    pool.wait_ge(rho_ready, i + 1)
                    pool.wait_ge(alpha_ready, u + 1)
                    if not first:
                        pool.wait_ge(summed, u + (1 - NG))
                    pool.tensor_tensor(mold[:, hs4], mnew[:, hs4].bitcast(F32), ones[:, 0:GH], ALU.mult
                                       ).then_inc(mold_ready, 1)
                    pool.tensor_tensor(Oacc[:, hs4, DH], Oacc[:, hs4, DH], alpha[:, hs4], ALU.mult)
                    for n in range(GH):
                        h = g * GH + n
                        ins = pool.tensor_scalar(Oacc[:, h, 0:DH], Oacc[:, h, 0:DH], alpha[:, h:h + 1], rho[:, 0:1],
                                                 ALU.mult, ALU.mult)
                    ins.then_inc(shrunk, 1)

            block_(0, first=True)
            with pool.Fori(1, NC) as i:
                block_(i)
            pool.wait_ge(pv_done, T_LAST)
            pool.memset(va, 1.0).then_inc(vone_ready, 1)

        @block.scalar
        def _(act):
            def root(n):
                act.wait_ge(var_ready, n + 1)
                nc.scalar.activation(vstd[:, 1:2], vstd[:, 0:1], ACT.Sqrt).then_inc(std_ready, 1)

            root(0)
            for g in range(4):
                act.wait_ge(wkT_ps, g + 1)
                nc.scalar.copy(WkT[:, 2 * g:2 * g + 2, :].rearrange("p j k -> p (j k)"), bk(g)).then_inc(wkT_ready, 1)

            def split_hi(i, p, first, at=5):
                n = tiles_of(p)
                if not first:
                    act.wait_ge(s_ready, i * STEPS + (2 * p + n - CT))
                    act.wait_ge(v_ready, i * RING + (2 * p + n - CT))
                act.wait_ge(tr_ready, i * PAIRS + (p + 1))
                nc.scalar.copy(ctxT[:, 2 * p:2 * p + n, 0, :, :].rearrange("p j k r -> p j (k r)"),
                               bk(at, n * D).rearrange("p (j n) -> p j n", j=n)).then_inc(ctxhi_ready, 1)

            def square(i, n):
                act.wait_ge(raw_loaded, i * 16 + 16)
                if n == 0 and not isinstance(i, int):
                    act.wait_ge(sq_ps, i)
                if not (isinstance(i, int) and i + n == 0):
                    act.wait_ge(sq_done, i * SQ + n)
                src = raw.rearrange("p j k -> p (j k)")[:, n * CT * D // SQ:(n + 1) * CT * D // SQ]
                nc.scalar.activation(squares, src, ACT.Square, accum_out=chsq[:, n:n + 1]).then_inc(sq_done, 1)

            for n in range(SQ):
                square(0, n)
            for p in range(PAIRS):
                split_hi(0, p, True, FIRST_BANKS[p])
            act.wait_ge(s_wv, 16)
            nc.scalar.copy(Wv_hi[:, :, :], Wv_sb).then_inc(wvhi_ready, 1)
            for n in range(2 * NG):
                act.wait_ge(A_ps, n + 1)
                nc.scalar.copy(A_hi[:, n // NG, n % NG * BANK:(n % NG + 1) * BANK], bk(n)).then_inc(Ahi_ready, 1)
            for n in range(3):
                act.wait_ge(wT_ps, n + 1)
                nc.scalar.copy(WqkvT.rearrange("p k n -> p (k n)")[:, n * BANK:(n + 1) * BANK],
                               bk(n)).then_inc(wT_ready, 1)
            act.wait_ge(wT_ps, 4)
            nc.scalar.copy(WoutT.rearrange("p k n -> p (k n)"), bk(3)).then_inc(wT_ready, 1)
            act.wait_ge(wT_ps, 5)
            nc.scalar.copy(gateT[:, :, :].rearrange("p k n -> p (k n)"), bk(4, KH * NE)).then_inc(wT_ready, 1)
            act.wait_ge(vone_ready, 1)
            act.wait_ge(ids, 5)
            act.wait_ge(wv_ready, 1)
            act.wait_ge(A_ready, 2 * NG)

            def block_(i, first=False, ahead=True, last=False):
                for k in range(STEPS if not last else EXP):
                    pair = None if last else pair_at(i, k, 1, first, ahead)
                    if pair:
                        split_hi(*pair, False)
                    if not last:
                        if not first or k >= RING:
                            act.wait_ge(d_ready, i * STEPS + (k + 1 - RING))
                        act.wait_ge(s_ready, i * STEPS + (k + 1))
                        nc.scalar.copy(ring[:, k % RING, :], bk(k % 2)).then_inc(copied, 1)
                        if k % 2 == 0:
                            half, j = k // RING, k % RING // 2
                            if k == 0:
                                act.wait_ge(sig_ready, i + 1)
                            if not first:
                                act.wait_ge(pv_done, i * STEPS + ((CT, 3 * CT)[half] + j + 1 - STEPS))
                            act.wait_ge(v_ready, i * RING + (k // 2 + 1))
                            nc.scalar.activation(V_hi[:, j, half * 8:half * 8 + 8, 0:DH],
                                                 values_at(k // 2).rearrange("p (h d) -> p h d", d=DH),
                                                 ACT.Copy, scale=sigma).then_inc(vhi_ready, 1)
                    if ahead and not last and SQ_STEP <= k < SQ_STEP + 2 * SQ and (k - SQ_STEP) % 2 == 0:
                        square(i + 1, (k - SQ_STEP) // 2)
                    u = late_unit(i, k, ROW, first, last)
                    if u:
                        act.wait_ge(mrow_ps, u[0] + 1)
                        nc.scalar.copy(mrow[u[1] % 2], bk(6)).then_inc(mrow_ready, 1)
                        act.wait_ge(fall_ready, u[0] + 1)
                        hs4 = slice(u[1] * GH, (u[1] + 1) * GH)
                        nc.scalar.activation(alpha[:, hs4], fall[:, hs4], ACT.Exp, scale=SCALE).then_inc(alpha_ready, 1)
                    s = late(i, k, EXP, first, last)
                    if s:
                        if not (first and s[1] < PR):
                            act.wait_ge(pv_done, s[0] + (1 - PR))
                        act.wait_ge(d_ready, s[0] + 1)
                        nc.scalar.activation(P_hi[:, s[1] % PR, :], dbuf[s[1] % 2], ACT.Exp,
                                             bias=lnp[:, 0:1], scale=SCALE).then_inc(phi_ready, 1)
                        if not (first and s[1] < 2):
                            act.wait_ge(p_ready, s[0] - 1)
                        nc.scalar.activation(pfull[s[1] % 2], dbuf[s[1] % 2], ACT.Exp,
                                             bias=lnp[:, 0:1], scale=SCALE).then_inc(exp_done, 1)

            block_(0, first=True)
            with act.Fori(1, NC - 1) as i:
                block_(i)
            block_(NC - 1, ahead=False)
            block_(NC, last=True)

            for n in range(2):
                act.wait_ge(OT_ps, n + 1)
                nc.scalar.copy(OT[:, 4 * n:4 * n + 4, :].rearrange("p j l -> p (j l)"), bk(n)).then_inc(OT_ready, 1)
            root(1)
            act.wait_ge(qkv_ps, 1)
            nc.scalar.copy(qkT.rearrange("p j n -> p (j n)"), bk(4)).then_inc(qkv_ready, 1)
            for n in range(8):
                skip_first(act, feat_ready, n - 1)
                if n % 2 == 0:
                    act.wait_ge(neg_ready, n // 2 + 1)
                    nc.scalar.activation(fexp[0], fneg[0], ACT.Exp).then_inc(fexp_ready, 1)
                else:
                    act.wait_ge(feat_ps, n + 1)
                    nc.scalar.activation(fneg[1], bk(n), ACT.Relu, scale=-1.0).then_inc(act_neg, 1)
                    act.wait_ge(act_neg, n // 2 + 1)
                    nc.scalar.activation(fexp[1], fneg[1], ACT.Exp, scale=-1.0).then_inc(fexp_ready, 1)
            root(2)
            act.wait_ge(xn_ready, 3)
            nc.scalar.copy(xn_split[:, 0, :], xn[:, :]).then_inc(xnhi_ready, 1)
            act.wait_ge(lmax_ready, 1)
            nc.scalar.activation(lg[:, 1, :], lg[:, 0, :], ACT.Exp, bias=small[:, 1:2],
                                 accum_out=small[:, 2:3]).then_inc(lexp_ready, 1)
            for n in range(2):
                act.wait_ge(disp_ps, n + 1)
                nc.scalar.copy(dispT[:, n, :], bk(n)).then_inc(disp_ready, 1)

            def half_of(t, a):
                return t[:, a * BANK:(a + 1) * BANK]

            def square_hidden(q):
                act.wait_ge(unit_used, up_done[q])
                for a in range(2):
                    skip_first(act, g_ready, 2 * (q - 2) + a + 1)
                    nc.scalar.activation(half_of(hg[q % 2], a), bank[q % 2][:, a, :], ACT.Square).then_inc(h2_ready, 1)

            square_hidden(0)
            act.wait_ge(combT_ps, 1)
            nc.scalar.copy(combT.rearrange("p q s -> p (q s)"), bk(7)).then_inc(combT_ready, 1)
            for q in range(NQ):
                for a in range(2):
                    act.wait_ge(u_ready, 2 * q + a + 1)
                    nc.scalar.activation(half_of(hg[q % 2], a), half_of(hh[q % 2], a), ACT.Tanh, scale=GELU_A
                                         ).then_inc(tanh_ready, 1)
                if q + 1 < NQ:
                    square_hidden(q + 1)
                if q > 0:
                    act.wait_ge(unit_used, down_done[q - 1])
                for a in range(2):
                    act.wait_ge(hT_ps, 2 * q + a + 1)
                    nc.scalar.mul(hT[:, a * FT // 2:(a + 1) * FT // 2, :].rearrange("p t n -> p (t n)"),
                                  bank[2][:, a, :], 0.5).then_inc(hT_ready, 1)

        @block.vector
        def _(dve_):
            steps = [0]

            def link(ins):
                steps[0] += 1
                ins.then_inc(dve, 1)
                dve_.wait_ge(dve, steps[0])

            v = nc.vector

            def layer_norm(n):
                link(v.bn_stats(st, x_sb[:, :]))
                link(v.bn_aggr(mv, st))
                v.tensor_scalar(vstd[:, 0:1], mv[:, 1:2], EPS, None, ALU.add).then_inc(var_ready, 1)
                dve_.wait_ge(std_ready, n + 1)
                link(v.reciprocal(vstd[:, 0:1], vstd[:, 1:2]))
                v.tensor_scalar(xn[:, :], x_sb[:, :], mv[:, 0:1], vstd[:, 0:1], ALU.subtract, ALU.mult
                                ).then_inc(xn_ready, 1)

            def take_xnT(n, i):
                dve_.wait_ge(xnT_ps, n + 1)
                v.tensor_copy(xnT[:, :, :].rearrange("p k l -> p (k l)"), bk(i, D)).then_inc(xnT_ready, 1)

            dve_.wait_ge(s_x, 16)
            layer_norm(0)
            take_xnT(0, 7)
            for n in range(2):
                dve_.wait_ge(q_ps, n + 1)
                v.tensor_copy(qT[:, 4 * n:4 * n + 4, :].rearrange("p j l -> p (j l)"), bk(4 + n)).then_inc(q_ready, 1)
            dve_.wait_ge(ids, 3)
            v.tensor_copy(iota_f[:, :], iota_i)
            v.tensor_copy(ones_r[:, :], ones[:, :])
            v.memset(mold[:, :], -3.0e38).then_inc(mold_ready, 1)
            def split_lo(i, p, at=5):
                n = tiles_of(p)
                dve_.wait_ge(ctxhi_ready, i * PAIRS + (p + 1))
                hi, lo = [ctxT[:, 2 * p:2 * p + n, s, :, :].rearrange("p j k r -> p j (k r)") for s in range(2)]
                v.tensor_tensor(lo, bk(at, n * D).rearrange("p (j n) -> p j n", j=n), hi.bitcast(F32),
                                ALU.subtract).then_inc(ctxlo_ready, 1)

            def take_squares(i, at=5):
                dve_.wait_ge(sq_ps, i + 1)
                v.tensor_reduce(bound[:, 0:1], bk(at, SQ), AX_X, ALU.add).then_inc(sig_own, 1)

            for p in range(PAIRS):
                split_lo(0, p, FIRST_BANKS[p])
            take_squares(0, 6)
            dve_.wait_ge(s_wv, 16)
            v.tensor_reduce(amax[:, 0:1], Wv_sb.rearrange("p k n -> p (k n)"), AX_X, ALU.max,
                            apply_absolute_value=True).then_inc(wmax_ready, 1)
            dve_.wait_ge(wvhi_ready, 1)
            v.tensor_tensor(Wv_lo[:, :, :], Wv_sb, Wv_hi[:, :, :].bitcast(F32), ALU.subtract).then_inc(wv_ready, 1)
            for n in range(2 * NG):
                sl = slice(n % NG * BANK, (n % NG + 1) * BANK)
                dve_.wait_ge(Ahi_ready, n + 1)
                v.tensor_tensor(A_lo[:, n // NG, sl], bk(n), A_hi[:, n // NG, sl].bitcast(F32), ALU.subtract
                                ).then_inc(A_ready, 1)

            dve_.wait_ge(gmax_ready, 1)
            link(v.tensor_tensor(wmax[:, 1:2], wmax[:, 0:1], wmax[:, 0:1], ALU.mult))

            def bound_values(i, n):
                dve_.wait_ge(sig_own, i * SIG_OWN + n)
                b = bound.bitcast(I32)
                if n == 1 and isinstance(i, int):
                    v.tensor_copy(bound[:, 1:2], bound[:, 0:1]).then_inc(sig_own, 1)
                elif n == 1:
                    v.tensor_tensor(bound[:, 1:2], bound[:, 1:2], bound[:, 0:1], ALU.add).then_inc(sig_own, 1)
                elif n == 2:
                    v.tensor_scalar(bound[:, 2:3], bound[:, 1:2], wmax[:, 1:2], 1e-30, ALU.mult, ALU.max
                                    ).then_inc(sig_own, 1)
                elif n == 3:
                    v.reciprocal(bound[:, 3:4], bound[:, 2:3]).then_inc(sig_own, 1)
                elif n == 4:
                    v.tensor_scalar(bound[:, 2:3], bound[:, 3:4], 2048.0 ** 2, None, ALU.mult).then_inc(sig_own, 1)
                elif n == 5:
                    v.tensor_scalar(b[:, 3:4], b[:, 2:3], 0x7F800000, 1, ALU.bitwise_and, ALU.logical_shift_right
                                    ).then_inc(sig_own, 1)
                else:
                    v.tensor_scalar(b[:, 2:3], b[:, 3:4], 127 << 22, None, ALU.add).then_inc(sig_own, 1)

            def scale_values(i):
                dve_.wait_ge(sig_own, i * SIG_OWN + SIG_OWN)
                v.tensor_scalar(sigma.bitcast(I32), bound[:, 2:3].bitcast(I32), 0x7F800000, None,
                                ALU.bitwise_and).then_inc(sig_ready, 1)

            for n in range(1, SIG_OWN):
                bound_values(0, n)
            scale_values(0)
            dve_.wait_ge(sig_ready, 1)
            v.reciprocal(sigma_inv, sigma).then_inc(inv_ready, 1)
            v.memset(rho, 1.0).then_inc(rho_ready, 1)

            def block_(i, first=False, ahead=True, last=False):
                for k in range(STEPS if not last else SUM - CT + 1):
                    pair = None if last else pair_at(i, k, 1, first, ahead)
                    if pair:
                        split_lo(*pair)
                    u = late_unit(i, k, MAX, first, last)
                    if u:
                        hs4 = slice(u[1] * GH, (u[1] + 1) * GH)
                        dve_.wait_ge(turned, u[0] + 1)
                        v.tensor_reduce(blkmax[:, hs4], bk(6).rearrange("p (h r) -> p h r", r=P), AX_X, ALU.max
                                        ).then_inc(blkmax_ready, 1)
                    s = late(i, k, LESS, first, last)
                    if s:
                        if not (first and s[1] < 2):
                            dve_.wait_ge(exp_done, s[0] - 1)
                        if s[1] % CT == 0:
                            dve_.wait_ge(mrow_ready, i * NG + ((k - LESS) // CT + 1))
                        v.tensor_tensor(dbuf[s[1] % 2], ring[:, s[1] % RING, :], mrow[s[1] // CT % 2], ALU.subtract
                                        ).then_inc(d_ready, 1)
                    if u:
                        dve_.wait_ge(blkmax_ready, u[0] + 1)
                        dve_.wait_ge(mold_ready, u[0] + 1)
                        v.tensor_tensor(mnew[:, hs4], mold[:, hs4], blkmax[:, hs4], ALU.max).then_inc(mnew_ready, 1)
                    g, j = k // CT, k % CT
                    if not last:
                        dve_.wait_ge(copied, i * STEPS + (k + 1))
                        if j:
                            if j == 1:
                                if not (first and g < 2):
                                    dve_.wait_ge(turned, i * NG + (g - 1))
                            else:
                                dve_.wait_ge(topped, i * (NG * (CT - 1)) + (g * (CT - 1) + j - 1))
                            v.tensor_tensor(tops[g % 2], ring[:, (k - 1) % RING, :] if j == 1 else tops[g % 2],
                                            ring[:, k % RING, :], ALU.max).then_inc(topped, 1)
                    if u:
                        dve_.wait_ge(mnew_ready, u[0] + 1)
                        if not (first and u[1] < 1):
                            dve_.wait_ge(mrow_ps, u[0])
                        v.tensor_tensor(diag[:, :, :], ident[:, :].unsqueeze(1).broadcast_to([P, GH, P]),
                                        mnew[:, hs4].bitcast(F32).unsqueeze(2).broadcast_to([P, GH, P]), ALU.mult
                                        ).then_inc(diag_ready, 1)
                    if not last:
                        if k == 0 and not first:
                            dve_.wait_ge(sig_ready, i + 1)
                        if k == RHO_STEP and not first:
                            dve_.wait_ge(shrunk, i * NG)
                            dve_.wait_ge(inv_ready, i)
                            v.tensor_tensor(rho, sigma, sigma_inv, ALU.mult).then_inc(rho_ready, 1)
                        if k == RHO_STEP + 1 and not first:
                            dve_.wait_ge(rho_ready, i + 1)
                            v.reciprocal(sigma_inv, sigma).then_inc(inv_ready, 1)
                        if k == SQ_SUM + 1 and ahead:
                            take_squares(i + 1)
                        if SQ_SUM + 1 < k <= SQ_SUM + SIG_OWN and ahead:
                            bound_values(i + 1, k - SQ_SUM - 1)
                        if k == STEPS - 1 and ahead:
                            dve_.wait_ge(vlo_ready, i * RING + RING)
                            scale_values(i + 1)
                        if k % 2 == 0:
                            half, jj = k // RING, k % RING // 2
                            dve_.wait_ge(vhi_ready, i * RING + (k // 2 + 1))
                            v.scalar_tensor_tensor(V_lo[:, jj, half * 8:half * 8 + 8, 0:DH],
                                                   values_at(k // 2).rearrange("p (h d) -> p h d", d=DH), sigma,
                                                   V_hi[:, jj, half * 8:half * 8 + 8, 0:DH], ALU.mult, ALU.subtract
                                                   ).then_inc(vlo_ready, 1)
                    s = late(i, k, LOW, first, last)
                    if s:
                        dve_.wait_ge(exp_done, s[0] + 1)
                        v.tensor_tensor(P_lo[:, s[1] % PR, :], pfull[s[1] % 2], P_hi[:, s[1] % PR, :], ALU.subtract
                                        ).then_inc(p_ready, 1)
                    u = late_unit(i, k, SUM, first, last)
                    if u:
                        dve_.wait_ge(pv_done, u[0] * CT + CT)
                        dve_.wait_ge(shrunk, u[0] + 1)
                        of_unit = Oacc[:, u[1] * GH:(u[1] + 1) * GH, 0:DH + 1]
                        v.tensor_tensor(of_unit, of_unit,
                                        bk(3 + u[1] % 2, GH * (DH + 1)).rearrange("p (h d) -> p h d", h=GH),
                                        ALU.add).then_inc(summed, 1)

            block_(0, first=True)
            with dve_.Fori(1, NC - 1) as i:
                block_(i)
            block_(NC - 1, ahead=False)
            block_(NC, last=True)

            dve_.wait_ge(summed, NC * NG)
            link(v.tensor_scalar(den[:, 0:H], Oacc[:, :, DH], sigma, None, ALU.mult))
            link(v.reciprocal(den[:, H:2 * H], den[:, 0:H]))
            for n in range(2):
                hs8 = slice(n * 8, n * 8 + 8)
                v.tensor_tensor(O.rearrange("p (h d) -> p h d", d=DH)[:, hs8], Oacc[:, hs8, 0:DH],
                                den[:, H + n * 8:H + n * 8 + 8].unsqueeze(2).broadcast_to([P, 8, DH]), ALU.mult
                                ).then_inc(O_ready, 1)
            dve_.wait_ge(xa_ps, 1)
            link(v.tensor_tensor(x_sb[:, :], x_sb[:, :], bk(2, D), ALU.add))

            layer_norm(1)
            take_xnT(1, 3)
            dve_.wait_ge(qkv_ps, 2)
            dve_.wait_ge(vone_ready, 2)
            v.tensor_copy(va[:, :, 0:HD], bk(5, D).rearrange("p (h d) -> p h d", d=HD)).then_inc(qkv_ready, 1)

            def negative(n):
                if n % 2 == 0:
                    skip_first(dve_, fexp_ready, n - 1)
                    dve_.wait_ge(feat_ps, n + 1)
                    v.tensor_scalar(fneg[n % 2], bk(n), 0.0, None, ALU.min).then_inc(neg_ready, 1)

            def feature(n):
                dst = (kp, qp)[n // 4][n % 4 // 2][:, n % 2 * BANK:(n % 2 + 1) * BANK]
                dve_.wait_ge(fexp_ready, n + 1)
                v.scalar_tensor_tensor(dst, bk(n), 0.0, fexp[n % 2], ALU.max, ALU.add).then_inc(feat_ready, 1)

            negative(0)
            for n in range(8):
                if n < 7:
                    negative(n + 1)
                feature(n)
            dve_.wait_ge(kv_ps, 1)
            v.tensor_copy(kv[:, :, 0:HD + 1], bk(0, H * (HD + 1)).rearrange("p (h d) -> p h d", d=HD + 1)
                          ).then_inc(kv_ready, 1)
            dve_.wait_ge(at_ps, 1)
            atp = bk(1, H * (HD + 1)).rearrange("p (h d) -> p h d", d=HD + 1)
            link(v.tensor_scalar(den[:, 0:H], atp[:, :, HD], 1e-8, None, ALU.add))
            link(v.reciprocal(den[:, H:2 * H], den[:, 0:H]))
            v.tensor_tensor(xn[:, :].rearrange("p (h d) -> p h d", d=HD), atp[:, :, 0:HD],
                            den[:, H:2 * H].unsqueeze(2).broadcast_to([P, H, HD]), ALU.mult).then_inc(at_ready, 1)
            dve_.wait_ge(atT_ps, 1)
            v.tensor_copy(xnT[:, :, :].rearrange("p k l -> p (k l)"), bk(2, D)).then_inc(atT_ready, 1)
            dve_.wait_ge(sa_ps, 1)
            link(v.tensor_tensor(x_sb[:, :], x_sb[:, :], bk(3, D), ALU.add))

            layer_norm(2)
            take_xnT(2, 4)
            dve_.wait_ge(xnhi_ready, 1)
            v.tensor_tensor(xn_split[:, 1, :], xn[:, :], xn_split[:, 0, :].bitcast(F32), ALU.subtract
                            ).then_inc(xnlo_ready, 1)
            dve_.wait_ge(lg_ps, 1)
            link(v.tensor_copy(lg[:, 0, :], bk(5, NE)))
            link(v.tensor_reduce(small[:, 0:1], lg[:, 0, :], AX_X, ALU.max))
            v.tensor_scalar(small[:, 1:2], small[:, 0:1], -1.0, None, ALU.mult).then_inc(lmax_ready, 1)
            link(v.tensor_scalar(lg[:, 2, :], lg[:, 0, :], small[:, 0:1], None, ALU.is_ge))
            link(v.scalar_tensor_tensor(lg[:, 3, :], lg[:, 2, :], -64.0, iota_f[:, 0:NE], ALU.mult, ALU.add))
            link(v.tensor_reduce(small[:, 4:5], lg[:, 3, :], AX_X, ALU.min))
            v.tensor_scalar(lg[:, 4, :], lg[:, 3, :], small[:, 4:5], None, ALU.is_equal).then_inc(mask_ready, 1)
            dve_.wait_ge(lexp_ready, 1)
            link(v.reciprocal(small[:, 3:4], small[:, 2:3]))
            link(v.tensor_scalar(lg[:, 1, :], lg[:, 1, :], small[:, 3:4], None, ALU.mult))
            dve_.wait_ge(rank_ps, 1)
            link(v.scalar_tensor_tensor(lg[:, 4, :], bk(6, NE), CAP + 0.5, lg[:, 4, :], ALU.is_lt, ALU.mult))
            link(v.scalar_tensor_tensor(lg[:, 5, :], bk(6, NE), -1.0, lg[:, 4, :], ALU.add, ALU.mult))
            link(v.tensor_reduce(small[:, 5:6], lg[:, 5, :], AX_X, ALU.add))
            link(v.tensor_tensor(lg[:, 6, :], lg[:, 4, :], lg[:, 1, :], ALU.mult))
            link(v.tensor_scalar(oh, iota_f[:, :], small[:, 5:6], None, ALU.is_equal))
            link(v.tensor_tensor(comb.rearrange("p (e c) -> p e c", c=CS),
                                 lg[:, 6, :].unsqueeze(2).broadcast_to([P, NE, CS]),
                                 oh.unsqueeze(1).broadcast_to([P, NE, CS]), ALU.mult))
            v.tensor_scalar(disp, comb, 0.0, None, ALU.is_gt).then_inc(comb_ready, 1)

            def inner(q):
                for a in range(2):
                    g, h = [t[q % 2][:, a * BANK:(a + 1) * BANK] for t in (hg, hh)]
                    dve_.wait_ge(h2_ready, 2 * q + a + 1)
                    link(v.tensor_scalar(g, g, GELU_B, 1.0, ALU.mult, ALU.add))
                    skip_first(dve_, hT_ps, 2 * (q - 2) + a + 1)
                    v.tensor_tensor(h, g, bank[q % 2][:, a, :], ALU.mult).then_inc(u_ready, 1)

            def gelu(q):
                for a in range(2):
                    g, h = [t[q % 2][:, a * BANK:(a + 1) * BANK] for t in (hg, hh)]
                    dve_.wait_ge(tanh_ready, 2 * q + a + 1)
                    v.scalar_tensor_tensor(h, g, 1.0, bank[q % 2][:, a, :], ALU.add, ALU.mult).then_inc(g_ready, 1)

            def take_y(q):
                skip_first(dve_, y_summed, q)
                dve_.wait_ge(unit_used, down_done[q])
                v.tensor_copy(y, bk(6, D)).then_inc(y_ready, 1)

            inner(0)
            for q in range(NQ):
                gelu(q)
                if q + 1 < NQ:
                    inner(q + 1)
                take_y(q)
            dve_.wait_ge(y_summed, NQ)
            v.tensor_tensor(res, x_sb[:, :], bk(7, D), ALU.add).then_inc(res_ready, 1)

        @block.tensor
        def _(pe):
            def mm(out_, lhsT, rhs, start=True, stop=True):
                return pe.matmul(out_, lhsT, rhs, start=start, stop=stop, skip_group_check=True)

            pe.wait_ge(ids, 1)
            pe.wait_ge(s_wk, 16)
            for g in range(4):
                for j in range(2 * g, 2 * g + 2):
                    for k in range(KH):
                        ins = pe.transpose(bk(g)[:, (j % 2 * KH + k) * P:(j % 2 * KH + k + 1) * P],
                                           Wk_sb[:, k, j * P:(j + 1) * P], ident[:, :])
                ins.then_inc(wkT_ps, 1)

            def transpose_tokens(n, i):
                pe.wait_ge(xn_ready, n + 1)
                for k in range(KH):
                    ins = pe.transpose(bk(i)[:, k * P:(k + 1) * P], xn[:, k * P:(k + 1) * P], ident[:, :])
                ins.then_inc(xnT_ps, 1)
                pe.wait_ge(xnT_ready, n + 1)

            transpose_tokens(0, 7)
            pe.wait_ge(s_wq, 16)
            for j in range(HP):
                for k in range(KH):
                    ins = mm(bk(4 + j // 4)[:, j % 4 * P:(j % 4 + 1) * P], Wq_sb[:, k, j * P:(j + 1) * P],
                             xnT[:, k, :], k == 0, k == KH - 1)
                if j % 4 == 3:
                    ins.then_inc(q_ps, 1)
            def turn(i, p, at=5):
                pe.wait_ge(raw_loaded, i * 16 + 16)
                if at == 5:
                    pe.wait_ge(*((ctxlo_ready, i * PAIRS + p) if p else (sig_own, i * SIG_OWN + 1)))
                for j in range(tiles_of(p)):
                    for k in range(KH):
                        ins = pe.transpose(bk(at)[:, (j * KH + k) * P:(j * KH + k + 1) * P],
                                           raw[:, 2 * p + j, k * P:(k + 1) * P], ident[:, :])
                ins.then_inc(tr_ready, 1)

            def sum_squares(i, at=5):
                if at == 5:
                    pe.wait_ge(ctxlo_ready, i * PAIRS)
                pe.wait_ge(sq_done, i * SQ + SQ)
                mm(bk(at, SQ), ones[:, :], chsq).then_inc(sq_ps, 1)

            pe.wait_ge(wkT_ready, 4)
            for p in range(PAIRS):
                turn(0, p, FIRST_BANKS[p])
            sum_squares(0, 6)
            pe.wait_ge(q_ready, 2)
            pe.wait_ge(sig_own, 1)
            pe.wait_ge(ctxlo_ready, PAIRS)
            for r in (0, DH):
                if r:
                    pe.wait_ge(A_even, 1)
                for k in range(KH):
                    for g in range(NG):
                        for h in range(g * GH + r // DH, (g + 1) * GH, 2):
                            ins = mm(bk(k * NG + g)[:, h % GH * P:(h % GH + 1) * P],
                                     WkT[r:r + DH, h // 2, k * P:(k + 1) * P], qT[r:r + DH, h // 2, :])
                        if r:
                            ins.then_inc(A_ps, 1)
                if not r:
                    ins.then_inc(A_even, 1)
            pe.wait_ge(s_tail, 16 * 9)
            for n in range(3):
                pe.wait_ge(A_ready, n + 1)
                for m in range(4 * n, 4 * n + 4):
                    ins = pe.transpose(bk(n)[:, m % 4 * P:(m % 4 + 1) * P],
                                       Wqkv_sb[m % 6][:, m // 6 * P:(m // 6 + 1) * P], ident[:, :])
                ins.then_inc(wT_ps, 1)
            pe.wait_ge(A_ready, 4)
            for k in range(KH):
                for r in range(2):
                    ins = pe.transpose(bk(3)[:, (k * 2 + r) * P:(k * 2 + r + 1) * P],
                                       Wout_sb[r][:, k * P:(k + 1) * P], ident[:, :])
            ins.then_inc(wT_ps, 1)
            pe.wait_ge(A_ready, 5)
            for k in range(KH):
                ins = pe.transpose(bk(4)[:, k * NE:(k + 1) * NE], gate_sb[:, k * P:(k + 1) * P], ident[0:NE, 0:NE])
            ins.then_inc(wT_ps, 1)
            pe.wait_ge(A_ready, 2 * NG)
            pe.wait_ge(wT_ready, 5)
            pe.wait_ge(wv_ready, 1)

            PARTS = ((0, 0), (0, 1), (1, 0))

            def values(i, n):
                if not (isinstance(i, int) and i == 0 and n < 2):
                    pe.wait_ge(vlo_ready, i * RING + (n - 1))
                half, j = n // CT, n % CT
                for m, (s, w) in enumerate(PARTS):
                    for k in range(KH):
                        ins = mm(values_at(n), ctxT[:, j, s, k, :], (Wv_hi, Wv_lo)[w][:, k, half * BANK:(half + 1) * BANK],
                                 m + k == 0, m + k == 3)
                ins.then_inc(v_ready, 1)

            def scores(i, k, first):
                g, j = k // CT, k % CT
                if g == 0:
                    pe.wait_ge(ctxlo_ready, i * PAIRS + (j // 2 + 1))
                if not (first and k < 2):
                    pe.wait_ge(copied, i * STEPS + (k - 1))
                for m, (s, w) in enumerate(PARTS):
                    for h in range(KH):
                        ins = mm(bk(k % 2), ctxT[:, j, s, h, :], (A_hi, A_lo)[w][:, h, g * BANK:(g + 1) * BANK],
                                 m + h == 0, m + h == 3)
                ins.then_inc(s_ready, 1)

            def weigh(i, b, first):
                g, j = b % STEPS // CT, b % CT
                pe.wait_ge(p_ready, i * STEPS + (b + 1))
                if g % 2 == 0:
                    pe.wait_ge(vlo_ready, i * RING + (b // STEPS * RING + g // 2 * CT + j + 1))
                if j == 0 and not (first and g < 2):
                    pe.wait_ge(summed, i * NG + (b // STEPS * NG + g - 1))
                r = b % PR
                for n in range(GH):
                    h = g * GH + n
                    hi, lo = P_hi[:, r, n * P:(n + 1) * P], P_lo[:, r, n * P:(n + 1) * P]
                    mm(acc_of(h), hi, V_hi[:, j, h, 0:DH + 1], j == 0 and n == 0, False)
                    mm(acc_of(h)[:, 0:DH], hi, V_lo[:, j, h, 0:DH], False, False)
                    ins = mm(acc_of(h), lo, V_hi[:, j, h, 0:DH + 1], False, False)
                ins.then_inc(pv_done, 1)

            def block_(i, first=False, ahead=True, last=False):
                for k in range(STEPS if not last else WEIGH + 2):
                    if not last:
                        if k == SQ_SUM and ahead:
                            sum_squares(i + 1)
                        pair = pair_at(i, k, 0, first, ahead)
                        if pair:
                            turn(*pair)
                        scores(i, k, first)
                    u = late_unit(i, k, DIAG, first, last)
                    if u:
                        pe.wait_ge(blkmax_ready, u[0] + 1)
                        pe.wait_ge(diag_ready, u[0] + 1)
                        mm(bk(6), ones_r[:, :], diag[:, :, :].rearrange("p h l -> p (h l)")).then_inc(mrow_ps, 1)
                    if not last:
                        if k % 2 == 0:
                            values(i, k // 2)
                    if k % BURST == BURST - 1:
                        for b in range(k - WEIGH - BURST + 1, k - WEIGH + 1):
                            if not (first and b < 0) and not (last and b >= 0):
                                weigh(i, b, first)
                    u = late_unit(i, k, TURN, first, last)
                    if u:
                        pe.wait_ge(topped, u[0] * (CT - 1) + (CT - 1))
                        if not (first and u[1] < 1):
                            pe.wait_ge(mrow_ready, u[0])
                        for n in range(GH):
                            ins = pe.transpose(bk(6)[:, n * P:(n + 1) * P], tops[u[1] % 2][:, n * P:(n + 1) * P], ident[:, :])
                        ins.then_inc(turned, 1)

            block_(0, first=True)
            with pe.Fori(1, NC - 1) as i:
                block_(i)
            block_(NC - 1, ahead=False)
            block_(NC, last=True)

            pe.wait_ge(s_rest, 16 * (2 + H))
            for j in range(HP):
                if j % 4 == 0:
                    pe.wait_ge(O_ready, j // 4 + 1)
                ins = pe.transpose(bk(j // 4)[:, j % 4 * P:(j % 4 + 1) * P], O[:, j * P:(j + 1) * P], ident[:, :])
                if j % 4 == 3:
                    ins.then_inc(OT_ps, 1)
            for j in range(HP):
                if j % 4 == 0:
                    pe.wait_ge(OT_ready, j // 4 + 1)
                ins = mm(bk(2, D), OT[:, j, :], Wo_sb[:, j, :], j == 0, j == HP - 1)
            ins.then_inc(xa_ps, 1)

            transpose_tokens(1, 3)
            for j in range(4):
                for k in range(KH):
                    ins = mm(bk(4)[:, j * P:(j + 1) * P], WqkvT[:, k, j * P:(j + 1) * P], xnT[:, k, :], k == 0, k == KH - 1)
            ins.then_inc(qkv_ps, 1)
            for k in range(KH):
                ins = mm(bk(5, D), xnT[:, k, :], WqkvT[:, k, 2 * D:3 * D], k == 0, k == KH - 1)
            ins.then_inc(qkv_ps, 1)
            pe.wait_ge(qkv_ready, 2)
            for n in range(4):
                mm(bk(n), qkT[:, 2 + n // 2, :], bd[:, n // 2, n % 2 * BANK:(n % 2 + 1) * BANK]).then_inc(feat_ps, 1)
            for n in range(4):
                for h in range(4 * n, 4 * n + 4):
                    ins = mm(bk(4 + n)[:, h % 4 * P:(h % 4 + 1) * P], bd[:, h // 8, h % 8 * F:(h % 8 + 1) * F],
                             qkT[:, h // 8, :])
                ins.then_inc(feat_ps, 1)
            for h in range(H):
                if h % 4 == 0:
                    pe.wait_ge(feat_ready, h // 4 + 1)
                ins = mm(bk(0)[:, h * (HD + 1):(h + 1) * (HD + 1)], kp[h // 8][:, h % 8 * F:(h % 8 + 1) * F],
                         va[:, h, 0:HD + 1])
            ins.then_inc(kv_ps, 1)
            pe.wait_ge(feat_ready, 8)
            pe.wait_ge(kv_ready, 1)
            for h in range(H):
                ins = mm(bk(1)[:, h * (HD + 1):(h + 1) * (HD + 1)], qp[h // 8][:, h % 8 * P:(h % 8 + 1) * P],
                         kv[:, h, 0:HD + 1])
            ins.then_inc(at_ps, 1)
            pe.wait_ge(at_ready, 1)
            for k in range(KH):
                ins = pe.transpose(bk(2)[:, k * P:(k + 1) * P], xn[:, k * P:(k + 1) * P], ident[:, :])
            ins.then_inc(atT_ps, 1)
            pe.wait_ge(atT_ready, 1)
            for k in range(KH):
                mm(bk(3, D), xnT[:, k, :], WoutT[:, k, :], k == 0, False)
            mm(bk(3, D), ones[0:1, :], b_sb[:, :], False, True).then_inc(sa_ps, 1)

            transpose_tokens(2, 4)
            for k in range(KH):
                ins = mm(bk(5, NE), xnT[:, k, :], gateT[:, k, :], k == 0, k == KH - 1)
            ins.then_inc(lg_ps, 1)
            pe.wait_ge(mask_ready, 1)
            mm(bk(6, NE), upper[:, :], lg[:, 4, :]).then_inc(rank_ps, 1)
            pe.wait_ge(comb_ready, 1)
            pe.wait_ge(xnlo_ready, 1)
            for k in range(KH):
                for s in (1, 0):
                    ins = mm(bk(k), xn_split[:, s, k * P:(k + 1) * P], disp, s == 1, s == 0)
                ins.then_inc(disp_ps, 1)
            pe.wait_ge(disp_ready, 2)

            done = [0]

            def next_unit():
                n = done[0]
                done[0] += 1
                pe.wait_ge(unit_loaded[n % UNITS], 16 * (n // UNITS + 1))
                return unit[n % UNITS]

            def up(q):
                skip_first(pe, g_ready, 2 * (q - 1))
                for j in range(QE):
                    w = next_unit().rearrange("p (k f) -> p k f", k=KH)
                    c0 = (q * QE + j) * CS
                    for half in range(2):
                        for k in range(KH):
                            ins = mm(bank[q % 2][j * CS:(j + 1) * CS, half, :], dispT[:, k, c0:c0 + CS],
                                     w[:, k, half * BANK:(half + 1) * BANK], k == 0, k == KH - 1)
                    ins.then_inc(unit_used, 1)

            def turn_hidden(q):
                for a in range(2):
                    pe.wait_ge(g_ready, 2 * q + a + 1)
                    skip_first(pe, hT_ready, 2 * (q - 1) + a + 1)
                    for t in range(a * FT // 2, (a + 1) * FT // 2):
                        ins = pe.transpose(bank[2][:, a, t % 4 * P:(t % 4 + 1) * P], hh[q % 2][:, t * P:(t + 1) * P],
                                           ident[:, :])
                    ins.then_inc(hT_ps, 1)

            def down(q):
                pe.wait_ge(hT_ready, 2 * q + 2)
                skip_first(pe, y_ready, q)
                for j in range(QE):
                    w = next_unit().rearrange("p (t d) -> p t d", t=FT)
                    for t in range(FT):
                        ins = mm(bk(6)[j * CS:(j + 1) * CS, 0:D], hT[:, t, j * CS:(j + 1) * CS], w[:, t, :],
                                 t == 0, t == FT - 1)
                    ins.then_inc(unit_used, 1)

            def combine(q):
                pe.wait_ge(y_ready, q + 1)
                pe.wait_ge(combT_ready, 1)
                mm(bk(7, D), combT[:, q, :], y, q == 0, q == NQ - 1).then_inc(y_summed, 1)

            up(0)
            for q in range(NQ):
                ins = pe.transpose(bk(7)[:, q * P:(q + 1) * P], comb[:, q * P:(q + 1) * P], ident[:, :])
            ins.then_inc(combT_ps, 1)
            for q in range(NQ):
                if q + 1 < NQ:
                    up(q + 1)
                turn_hidden(q)
                if q > 0:
                    combine(q - 1)
                down(q)
            combine(NQ - 1)


_INS = ["x", "ctx_1024", "L0_xattn_Wq", "L0_xattn_Wk", "L0_xattn_Wv", "L0_xattn_Wo", "L0_attn_W_qkv",
        "L0_attn_proj", "L0_attn_W_out", "L0_attn_b_out", "L0_ffn_gate_w", "L0_ffn_w1", "L0_ffn_w2"]
_OUTS = [((1, 128, 256), "float32")]


def kernel(**inputs):
    import numpy as _np
    import concourse.bacc as _bacc
    from concourse import mybir as _mybir
    from concourse.bass_utils import run_bass_kernel_spmd as _run

    nc = _bacc.Bacc("TRN2", target_bir_lowering=False, num_devices=1)
    arrays, args = {}, []
    for name in _INS:
        a = _np.ascontiguousarray(inputs[name])
        arrays[f"in_{name}_dram"] = a
        args.append(nc.dram_tensor(f"in_{name}_dram", a.shape, _mybir.dt.from_np(a.dtype), kind="ExternalInput").ap())
    for i, (shape, dtype) in enumerate(_OUTS):
        dt = _mybir.dt.from_np(_np.dtype(dtype))
        args.append(nc.dram_tensor(f"out_{i}_dram", shape, dt, kind="ExternalOutput").ap())
    perceiver_layer(nc, *args)
    r = _run(nc, [arrays], core_ids=[0])
    got = tuple(r.results[0][f"out_{i}_dram"] for i in range(len(_OUTS)))
    return got[0]
```
